# Optimizing a Trainium2 kernel written in Bass

```python
import numpy as np
import jax
import jax.numpy as jnp

def _softmax(x, axis=-1):
    return jax.nn.softmax(x, axis=axis)

def _gelu(x):
    return jax.nn.gelu(x, approximate=True)

def _silu(x):
    return jax.nn.silu(x)

def _sigmoid(x):
    return jax.nn.sigmoid(x)

def _layernorm(x, axis=-1, eps=1e-05):
    m = jnp.mean(x, axis=axis, keepdims=True)
    v = jnp.var(x, axis=axis, keepdims=True)
    return (x - m) / jnp.sqrt(v + eps)

def _scatter_add(tgt, idx, src, axis=0):
    return tgt.at[idx].add(src)

def _segment_sum(src, seg, n):
    return jax.ops.segment_sum(src, seg, n)
kernel_name = 'mk_gnn_preln_d1_gnn_r8_674e66'

def setup_inputs(seed: int=0):
    np.random.seed(seed)
    _w = jnp.asarray

    def _rec_inputs():
        import jax
        import jax.numpy as jnp
        _gk = jax.random.key(seed)
        x = -0.0004942 + 1 * jax.random.normal(jax.random.fold_in(_gk, 1), (6250, 128), jnp.float32)
        src = jax.random.randint(jax.random.fold_in(_gk, 2), (200000,), 0, 6250, jnp.int32)
        dst = jnp.minimum((6250 * jax.random.uniform(jax.random.fold_in(_gk, 3), (200000,)) ** 2.0).astype(jnp.int32), 49999)
        _o = jnp.argsort(dst, stable=True)
        src = src[_o]
        dst = dst[_o]
        edge_attr_4 = 0.00132558 + 1.00026 * jax.random.normal(jax.random.fold_in(_gk, 12), (200000, 4), jnp.float32)
        return (x, src, dst, edge_attr_4)
    x, src, dst, edge_attr_4 = _rec_inputs()

    def _L0_gnn_setup():
        import jax, jax.numpy as jnp
        import numpy as np
        N, E, D, H, HD, TD, ED, G = (3750, 60000, 128, 8, 16, 512, 4, 8)

        def group_norm(x, gamma, beta, num_groups=G, eps=1e-05):
            n, c = x.shape
            xr = x.reshape(n, num_groups, c // num_groups)
            mu = xr.mean(-1, keepdims=True)
            var = ((xr - mu) ** 2).mean(-1, keepdims=True)
            xn = (xr - mu) * jax.lax.rsqrt(var + eps)
            return xn.reshape(n, c) * gamma + beta

        def mesh_conv(x, src, dst, ea, w1, b1, g, bt, w2, b2):
            m = jnp.concatenate([x[dst], x[src], ea], axis=-1) @ w1 + b1
            m = jax.nn.silu(group_norm(m, g, bt))
            m = m @ w2 + b2
            n = x.shape[0]
            out = jax.ops.segment_sum(m, dst, num_segments=n)
            cnt = jax.ops.segment_sum(jnp.ones((dst.shape[0],), m.dtype), dst, num_segments=n)
            return out / jnp.clip(cnt, 1.0)[:, None]
        key = jax.random.key(seed)
        ks = jax.random.split(key, 32)
        inp = {}
        inp['x'] = jax.random.normal(ks[0], (N, D), jnp.float32)
        inp['edge_src'] = jax.random.randint(ks[1], (E,), 0, N, jnp.int32)
        inp['edge_dst'] = jax.random.randint(ks[2], (E,), 0, N, jnp.int32)
        inp['edge_attr'] = jax.random.normal(ks[3], (E, ED), jnp.float32)
        inp['t_emb'] = jax.random.normal(ks[4], (TD,), jnp.float32)
        s = 0.02
        inp['c1_w1'] = jax.random.normal(ks[5], (2 * D + ED, D)) * s
        inp['c1_b1'] = jnp.zeros((D,))
        inp['c1_g'] = jnp.ones((D,))
        inp['c1_bt'] = jnp.zeros((D,))
        inp['c1_w2'] = jax.random.normal(ks[6], (D, D)) * s
        inp['c1_b2'] = jnp.zeros((D,))
        inp['c2_w1'] = jax.random.normal(ks[7], (2 * D + ED, D)) * s
        inp['c2_b1'] = jnp.zeros((D,))
        inp['c2_g'] = jnp.ones((D,))
        inp['c2_bt'] = jnp.zeros((D,))
        inp['c2_w2'] = jax.random.normal(ks[8], (D, D)) * s
        inp['c2_b2'] = jnp.zeros((D,))
        inp['tm_w'] = jax.random.normal(ks[9], (TD, D)) * s
        inp['tm_b'] = jnp.zeros((D,))
        inp['n1_g'] = jnp.ones((D,))
        inp['n1_b'] = jnp.zeros((D,))
        inp['n2_g'] = jnp.ones((D,))
        inp['n2_b'] = jnp.zeros((D,))
        inp['qw'] = jax.random.normal(ks[10], (D, D)) * s
        inp['qb'] = jnp.zeros((D,))
        inp['kw'] = jax.random.normal(ks[11], (D, D)) * s
        inp['kb'] = jnp.zeros((D,))
        inp['vw'] = jax.random.normal(ks[12], (D, D)) * s
        inp['vb'] = jnp.zeros((D,))
        inp['ew'] = jax.random.normal(ks[13], (ED, H)) * s
        inp['eb'] = jnp.zeros((H,))
        inp['ow'] = jax.random.normal(ks[14], (D, D)) * s
        inp['ob'] = jnp.zeros((D,))
        inp['an_g'] = jnp.ones((D,))
        inp['an_b'] = jnp.zeros((D,))
        return inp
    _L0_gnn_all = _L0_gnn_setup()
    _L0_gnn_in = {k: v for k, v in _L0_gnn_all.items() if k in ('t_emb', 'c1_w1', 'c1_b1', 'c1_g', 'c1_bt', 'c1_w2', 'c1_b2', 'c2_w1', 'c2_b1', 'c2_g', 'c2_bt', 'c2_w2', 'c2_b2', 'tm_w', 'tm_b', 'n1_g', 'n1_b', 'n2_g', 'n2_b', 'qw', 'qb', 'kw', 'kb', 'vw', 'vb', 'ew', 'eb', 'ow', 'ob', 'an_g', 'an_b')}
    del _L0_gnn_all
    return {'x': x, 'src': src, 'dst': dst, 'edge_attr_4': edge_attr_4, 'L0_gnn_t_emb': _L0_gnn_in['t_emb'], 'L0_gnn_c1_w1': _L0_gnn_in['c1_w1'], 'L0_gnn_c1_b1': _L0_gnn_in['c1_b1'], 'L0_gnn_c1_g': _L0_gnn_in['c1_g'], 'L0_gnn_c1_bt': _L0_gnn_in['c1_bt'], 'L0_gnn_c1_w2': _L0_gnn_in['c1_w2'], 'L0_gnn_c1_b2': _L0_gnn_in['c1_b2'], 'L0_gnn_c2_w1': _L0_gnn_in['c2_w1'], 'L0_gnn_c2_b1': _L0_gnn_in['c2_b1'], 'L0_gnn_c2_g': _L0_gnn_in['c2_g'], 'L0_gnn_c2_bt': _L0_gnn_in['c2_bt'], 'L0_gnn_c2_w2': _L0_gnn_in['c2_w2'], 'L0_gnn_c2_b2': _L0_gnn_in['c2_b2'], 'L0_gnn_tm_w': _L0_gnn_in['tm_w'], 'L0_gnn_tm_b': _L0_gnn_in['tm_b'], 'L0_gnn_n1_g': _L0_gnn_in['n1_g'], 'L0_gnn_n1_b': _L0_gnn_in['n1_b'], 'L0_gnn_n2_g': _L0_gnn_in['n2_g'], 'L0_gnn_n2_b': _L0_gnn_in['n2_b'], 'L0_gnn_qw': _L0_gnn_in['qw'], 'L0_gnn_qb': _L0_gnn_in['qb'], 'L0_gnn_kw': _L0_gnn_in['kw'], 'L0_gnn_kb': _L0_gnn_in['kb'], 'L0_gnn_vw': _L0_gnn_in['vw'], 'L0_gnn_vb': _L0_gnn_in['vb'], 'L0_gnn_ew': _L0_gnn_in['ew'], 'L0_gnn_eb': _L0_gnn_in['eb'], 'L0_gnn_ow': _L0_gnn_in['ow'], 'L0_gnn_ob': _L0_gnn_in['ob'], 'L0_gnn_an_g': _L0_gnn_in['an_g'], 'L0_gnn_an_b': _L0_gnn_in['an_b']}

def reference(x, src, dst, edge_attr_4, L0_gnn_t_emb, L0_gnn_c1_w1, L0_gnn_c1_b1, L0_gnn_c1_g, L0_gnn_c1_bt, L0_gnn_c1_w2, L0_gnn_c1_b2, L0_gnn_c2_w1, L0_gnn_c2_b1, L0_gnn_c2_g, L0_gnn_c2_bt, L0_gnn_c2_w2, L0_gnn_c2_b2, L0_gnn_tm_w, L0_gnn_tm_b, L0_gnn_n1_g, L0_gnn_n1_b, L0_gnn_n2_g, L0_gnn_n2_b, L0_gnn_qw, L0_gnn_qb, L0_gnn_kw, L0_gnn_kb, L0_gnn_vw, L0_gnn_vb, L0_gnn_ew, L0_gnn_eb, L0_gnn_ow, L0_gnn_ob, L0_gnn_an_g, L0_gnn_an_b):
    import jax
    import jax.numpy as jnp

    def _L0_gnn_ref(x, edge_src, edge_dst, edge_attr, t_emb, c1_w1, c1_b1, c1_g, c1_bt, c1_w2, c1_b2, c2_w1, c2_b1, c2_g, c2_bt, c2_w2, c2_b2, tm_w, tm_b, n1_g, n1_b, n2_g, n2_b, qw, qb, kw, kb, vw, vb, ew, eb, ow, ob, an_g, an_b):
        import jax, jax.numpy as jnp
        import numpy as np
        N, E, D, H, HD, TD, ED, G = (3750, 60000, 128, 8, 16, 512, 4, 8)

        def group_norm(x, gamma, beta, num_groups=G, eps=1e-05):
            n, c = x.shape
            xr = x.reshape(n, num_groups, c // num_groups)
            mu = xr.mean(-1, keepdims=True)
            var = ((xr - mu) ** 2).mean(-1, keepdims=True)
            xn = (xr - mu) * jax.lax.rsqrt(var + eps)
            return xn.reshape(n, c) * gamma + beta

        def mesh_conv(x, src, dst, ea, w1, b1, g, bt, w2, b2):
            m = jnp.concatenate([x[dst], x[src], ea], axis=-1) @ w1 + b1
            m = jax.nn.silu(group_norm(m, g, bt))
            m = m @ w2 + b2
            n = x.shape[0]
            out = jax.ops.segment_sum(m, dst, num_segments=n)
            cnt = jax.ops.segment_sum(jnp.ones((dst.shape[0],), m.dtype), dst, num_segments=n)
            return out / jnp.clip(cnt, 1.0)[:, None]
        src, dst = (edge_src, edge_dst)
        n = x.shape[0]
        h = mesh_conv(x, src, dst, edge_attr, c1_w1, c1_b1, c1_g, c1_bt, c1_w2, c1_b2)
        h = jax.nn.silu(group_norm(h, n1_g, n1_b))
        h = h + (jax.nn.silu(t_emb) @ tm_w + tm_b)
        h = mesh_conv(h, src, dst, edge_attr, c2_w1, c2_b1, c2_g, c2_bt, c2_w2, c2_b2)
        h = jax.nn.silu(group_norm(h, n2_g, n2_b))
        h = h + x
        q = (h @ qw + qb).reshape(n, H, HD)
        k = (h @ kw + kb).reshape(n, H, HD)
        v = (h @ vw + vb).reshape(n, H, HD)
        scale = HD ** (-0.5)
        logits = (q[dst] * k[src]).sum(-1) * scale + (edge_attr @ ew + eb)
        amax = jax.ops.segment_max(logits, dst, num_segments=n)
        pe = jnp.exp(logits - amax[dst])
        ssum = jax.ops.segment_sum(pe, dst, num_segments=n)
        w = pe / jnp.clip(ssum[dst], 1e-06)
        o = jax.ops.segment_sum(w[:, :, None] * v[src], dst, num_segments=n)
        o = o.reshape(n, D) @ ow + ob
        o = group_norm(o, an_g, an_b)
        return h + o
    h = jnp.maximum(_layernorm(x, axis=-1), 0.0)
    x = x + _L0_gnn_ref(h, src, dst, edge_attr_4, L0_gnn_t_emb, L0_gnn_c1_w1, L0_gnn_c1_b1, L0_gnn_c1_g, L0_gnn_c1_bt, L0_gnn_c1_w2, L0_gnn_c1_b2, L0_gnn_c2_w1, L0_gnn_c2_b1, L0_gnn_c2_g, L0_gnn_c2_bt, L0_gnn_c2_w2, L0_gnn_c2_b2, L0_gnn_tm_w, L0_gnn_tm_b, L0_gnn_n1_g, L0_gnn_n1_b, L0_gnn_n2_g, L0_gnn_n2_b, L0_gnn_qw, L0_gnn_qb, L0_gnn_kw, L0_gnn_kb, L0_gnn_vw, L0_gnn_vb, L0_gnn_ew, L0_gnn_eb, L0_gnn_ow, L0_gnn_ob, L0_gnn_an_g, L0_gnn_an_b)
    return x

_drawn_inputs = setup_inputs


def setup_inputs(seed=0):
    import zlib

    import numpy as np

    out = dict(_drawn_inputs(seed))
    spreads = {'L0_gnn_c1_b1': (0.0, 0.1),
     'L0_gnn_c1_g': (1.0, 0.2),
     'L0_gnn_c1_bt': (0.0, 0.481),
     'L0_gnn_c1_b2': (0.0, 0.1),
     'L0_gnn_c2_b1': (0.0, 0.1),
     'L0_gnn_c2_g': (1.0, 0.2),
     'L0_gnn_c2_bt': (0.0, 0.303),
     'L0_gnn_c2_b2': (0.0, 0.1),
     'L0_gnn_tm_b': (0.0, 0.1),
     'L0_gnn_n1_g': (1.0, 0.2),
     'L0_gnn_n1_b': (0.0, 0.34),
     'L0_gnn_n2_g': (1.0, 0.2),
     'L0_gnn_n2_b': (0.0, 0.1),
     'L0_gnn_qb': (0.0, 0.8),
     'L0_gnn_kb': (0.0, 2.0),
     'L0_gnn_vb': (0.0, 0.1),
     'L0_gnn_eb': (0.0, 2.0),
     'L0_gnn_ob': (0.0, 0.1),
     'L0_gnn_an_g': (1.0, 0.2),
     'L0_gnn_an_b': (0.0, 0.1)}
    factors = {'edge_attr_4': 4.46, 'L0_gnn_qw': 8.0, 'L0_gnn_kw': 8.0, 'L0_gnn_ew': 8.0}
    for name, (base, spread) in spreads.items():
        noise = np.random.default_rng([zlib.crc32(name.encode()), seed]).standard_normal(out[name].shape)
        drawn = base * np.exp(spread * noise) if base else spread * noise
        out[name] = jnp.asarray(drawn.astype(out[name].dtype))
    for name, factor in factors.items():
        out[name] = (out[name] * factor).astype(out[name].dtype)
    return out
```

```python
from contextlib import ExitStack

import numpy as np
import concourse.bass as bass
from concourse import mybir

F32 = mybir.dt.float32
BF16 = mybir.dt.bfloat16
I32 = mybir.dt.int32
ALU = mybir.AluOpType
ACT = mybir.ActivationFunctionType
AX = mybir.AxisListType

P = 128
N_NODES, N_EDGES, D = 6250, 200000, 128
HEADS, GROUPS, ED, TD = 8, 8, 4, 512
HD = D // HEADS
GC = D // GROUPS
BLOCKS = -(-N_NODES // P)
NODES = BLOCKS * P
TILES = 4
SUPER = TILES * P
DEPTH = 4
ITERS = -(-N_EDGES // (DEPTH * SUPER))
SUPERS = DEPTH * ITERS
EDGES = SUPERS * SUPER
CHUNK = 7
CHUNKS = BLOCKS // CHUNK
WIN = P // HEADS
WINDOWS = NODES // WIN
ACC_W = D + HEADS
TAB_P = SUPERS // 4
EPS = 1e-5
EA_SPLIT = P // ED
EA_COLS = EDGES // EA_SPLIT
CC = CHUNK * D
NEG = -1e30
RANGE_AT = (0, 6, 12, 21)
RANGE_BITS = (6, 6, 9, 9)
ROOT_SEED = 0x5f3759df
ROOT = (-5.148723380996802, 10.818224541572237, -12.019660736923178, 9.008935881668528)
ROOT_K = 0.2733154241963853
ROOT_STEPS = 8
PEN = 2.0 ** 50
assert CHUNKS * CHUNK == BLOCKS and TAB_P * 4 == SUPERS


def wait(eng, sem, value):
    if isinstance(value, int) and value <= 0:
        return
    eng.wait_ge(sem, value)


def hold(eng, sem, value, paced):
    if isinstance(value, int) and value <= 0:
        return
    eng.wait_ge(sem, value)
    eng.sem_inc(paced, 1)


def slots(eng, last_lag, body):
    def turn(i):
        for h in range(DEPTH):
            def stage(lag, h=h):
                back, r = divmod(h - lag, DEPTH)
                k = i + back
                if isinstance(k, int) and not 0 <= k < ITERS:
                    return None
                return DEPTH * k + r, r, k
            body(stage)

    tail = -(-last_lag // DEPTH)
    for i in range(tail + 1):
        turn(i)
    with eng.Fori(tail + 1, ITERS) as i:
        turn(i)
    for i in range(ITERS, ITERS + tail):
        turn(i)


def build(nc, io, out):
    ctx = ExitStack()
    with ctx:
        def sb(name, shape, dt=F32):
            return ctx.enter_context(nc.sbuf_tensor(name, shape, dt))

        live = []

        def sem(name):
            live.append(nc.alloc_semaphore(name))
            return live[-1]

        def end_phase():
            nc.clear_and_free_semaphores(live)
            live.clear()
            nc.all_engine_barrier()

        def dram(name, shape, dt=F32):
            return nc.dram_tensor(name, shape, dt, kind="Internal").ap()

        resid = dram("resid", [NODES, D])
        src_table = dram("src_table", [NODES, 3 * D], BF16)
        kv_table = dram("kv_table", [NODES, 2 * D])
        dst_rows = dram("dst_rows", [SUPERS, SUPER])
        dst_digits = dram("dst_digits", [2, EDGES], BF16)
        ea_parts = dram("ea_parts", [9 * ED, EDGES], BF16)
        w_parts_d = dram("w_parts_d", [2, 3 * ED, D], BF16)
        ranges_d = dram("ranges_d", [SUPERS], I32)
        v_edges = dram("v_edges", [SUPERS, P, TILES * D])
        max_nodes = dram("max_nodes", [NODES, HEADS])

        ps = ctx.enter_context(nc.psum_tensor("ps", [P, 8, 512], F32))

        def bank(k):
            return ps[:, k, :]

        def banks(k, cols):
            return ps[:, k:k + 2, :].rearrange("p a b -> p (a b)")[:, 0:cols]

        ident, ident_b = sb("ident", [P, P]), sb("ident_b", [P, P], BF16)
        iota_row = sb("iota_row", [P, P])
        node_of = sb("node_of", [P, BLOCKS])
        neg_block = sb("neg_block", [P, BLOCKS])
        win_node = sb("win_node", [P, WINDOWS + 1])
        ranges = sb("ranges", [1, SUPERS], I32)
        dst_cols = sb("dst_cols", [P, SUPERS * TILES])
        digit_w = sb("digit_w", [2, P], BF16)
        neg_node = sb("neg_node", [P, BLOCKS])
        neg_win = sb("neg_win", [P, WINDOWS + 1])
        one_col = sb("one_col", [P, 1])
        dst_parts = sb("dst_parts", [P, BLOCKS, 3, D], BF16)
        acc = sb("acc", [P, BLOCKS, ACC_W])
        hidden = sb("hidden", [P, BLOCKS, D])
        w_pair = [sb(f"w_pair{n}", [P, 2, D]) for n in range(2)]
        w_edge = [sb(f"w_edge{n}", [9 * ED, D], BF16) for n in range(2)]
        b1_row = [sb(f"b1_row{n}", [P, D]) for n in range(2)]
        w_qkv, b_qkv = sb("w_qkv", [P, 3, D]), [sb(f"b_qkv{r}", [P, D]) for r in range(3)]
        tvec = sb("tvec", [P, D])
        eps_col = sb("eps_col", [P, 1])

        def row_vector(name):
            return io[name].rearrange("(a n) -> a n", a=1).to_broadcast([P, D])

        def by_block(table, i):
            return table.rearrange("(b p) c -> p b c", p=P)[:, bass.ds(CHUNK * i, CHUNK), :]

        def row_of(row):
            return row[:, :].unsqueeze(1).to_broadcast([P, CHUNK, D])

        def chain(eng, step, base):
            count = [0]

            def done(ins):
                count[0] += 1
                ins.then_inc(step, 1)
                eng.wait_ge(step, base + count[0])
            return done

        def split_parts(dve, done, rest, to):
            for part in range(3):
                done(dve.tensor_copy(to[part], rest))
                if part < 2:
                    done(dve.tensor_tensor(rest, rest, to[part], ALU.subtract))

        def root_steps(dve, v, y, t, p):
            a, b_, c, d = ROOT
            return (lambda: dve.tensor_scalar(v, v, EPS, None, ALU.add),
                    lambda: dve.tensor_scalar(y.bitcast(I32), v.bitcast(I32), -0.5, float(ROOT_SEED), ALU.mult, ALU.add),
                    lambda: dve.tensor_tensor(t, y, y, ALU.mult),
                    lambda: dve.tensor_tensor(t, t, v, ALU.mult),
                    lambda: dve.scalar_tensor_tensor(p, t, a, t, ALU.add, ALU.mult),
                    lambda: dve.scalar_tensor_tensor(p, p, b_, t, ALU.add, ALU.mult),
                    lambda: dve.scalar_tensor_tensor(p, p, c, t, ALU.add, ALU.mult),
                    lambda: dve.scalar_tensor_tensor(y, p, d, y, ALU.add, ALU.mult))

        st = ExitStack()
        pid_i = st.enter_context(nc.sbuf_tensor("pid_i", [P, 1], I32))
        pid_f = st.enter_context(nc.sbuf_tensor("pid_f", [P, 1], F32))
        iota_i = st.enter_context(nc.sbuf_tensor("iota_i", [P, P], I32))
        node_i = st.enter_context(nc.sbuf_tensor("node_i", [P, BLOCKS], I32))
        negb_i = st.enter_context(nc.sbuf_tensor("negb_i", [P, BLOCKS], I32))
        win_i = st.enter_context(nc.sbuf_tensor("win_i", [P, WINDOWS + 1], I32))
        lane_i = st.enter_context(nc.sbuf_tensor("lane_i", [P, 1], I32))
        lane_f = st.enter_context(nc.sbuf_tensor("lane_f", [P, 1], F32))
        rows_i = st.enter_context(nc.sbuf_tensor("rows_i", [TAB_P, 4 * SUPER], I32))
        digit_i = st.enter_context(nc.sbuf_tensor("digit_i", [TAB_P, 2, 4 * SUPER], I32))
        digit_b = st.enter_context(nc.sbuf_tensor("digit_b", [TAB_P, 2, 4 * SUPER], BF16))
        rows_f = st.enter_context(nc.sbuf_tensor("rows_f", [TAB_P, 4, SUPER], F32))
        ends_f = st.enter_context(nc.sbuf_tensor("ends_f", [TAB_P, 4, 2], F32))
        ends_i = st.enter_context(nc.sbuf_tensor("ends_i", [TAB_P, 4, 2], I32))
        range_i = st.enter_context(nc.sbuf_tensor("range_i", [TAB_P, 4, 4], I32))
        range_f = st.enter_context(nc.sbuf_tensor("range_f", [TAB_P, 4, 4], F32))
        range_o = st.enter_context(nc.sbuf_tensor("range_o", [TAB_P, 4, 4], I32))
        word = st.enter_context(nc.sbuf_tensor("word", [TAB_P, 4], I32))
        cols_i = st.enter_context(nc.sbuf_tensor("cols_i", [P, SUPERS * TILES], I32))
        w_raw = st.enter_context(nc.sbuf_tensor("w_raw", [P, 8, D], F32))
        w_mean = st.enter_context(nc.sbuf_tensor("w_mean", [P, 8, GROUPS], F32))
        w_edge_f = st.enter_context(nc.sbuf_tensor("w_edge_f", [ED, 2, D], F32))
        w_edge_b = st.enter_context(nc.sbuf_tensor("w_edge_b", [ED, 2, 3, D], BF16))
        ea_f = acc[:, :, :].rearrange("p b c -> p (b c)")[:, 0:EA_COLS]
        ea_b = dst_parts[:, :, :, :].rearrange("p b k c -> p (b k c)").rearrange("p (a e) -> p a e", a=3)
        with st:
            iota_done, dst_in, weights_in, step = sem("iota_done"), sem("dst_in"), sem("weights_in"), sem("setup_step")
            digits_out, ranges_out, ranges_in = sem("digits_out"), sem("ranges_out"), sem("ranges_in")
            rows_out, ea_in, ea_cut, ea_left, ea_out = (sem(x) for x in ("rows_out", "ea_in", "ea_cut", "ea_left", "ea_out"))
            w_split, w_out, w_edge_in = (sem(x) for x in ("w_split", "w_out", "w_edge_in"))
            with nc.Block() as block:
                @block.gpsimd
                def _(pool):
                    pool.iota(pid_i[:, :], [[0, 1]], base=0, channel_multiplier=1).then_inc(iota_done, 1)
                    pool.iota(iota_i[:, :], [[1, P]], base=0, channel_multiplier=0).then_inc(iota_done, 1)
                    pool.iota(node_i[:, :], [[P, BLOCKS]], base=0, channel_multiplier=1).then_inc(iota_done, 1)
                    pool.iota(negb_i[:, :], [[-P, BLOCKS]], base=0, channel_multiplier=0).then_inc(iota_done, 1)
                    pool.iota(win_i[:, :], [[WIN, WINDOWS + 1]], base=0, channel_multiplier=0).then_inc(iota_done, 1)

                @block.sync
                def _(sp):
                    sp.dma_start(rows_i[:, :], io["dst_rows"].rearrange("(p c) e -> p (c e)", c=4)).then_inc(dst_in, 16)
                    sp.dma_start(cols_i[:, :], io["dst_cols"]).then_inc(dst_in, 16)
                    sp.dma_start(ea_f, io["ea_rows"].rearrange("c (q e) -> (c q) e", q=EA_SPLIT)).then_inc(ea_in, 16)
                    for n in range(2):
                        w1 = io[f"L0_gnn_c{n + 1}_w1"]
                        for half in range(2):
                            sp.dma_start(w_raw[:, 4 * n + half, :], w1[half * D:(half + 1) * D, :]).then_inc(weights_in, 16)
                        sp.dma_start(w_raw[0:ED, 4 * n + 2, :], w1[2 * D:2 * D + ED, :]).then_inc(weights_in, 16)
                        sp.dma_start(w_raw[:, 4 * n + 3, :], row_vector(f"L0_gnn_c{n + 1}_b1")).then_inc(weights_in, 16)
                    for r, x in enumerate("qkv"):
                        sp.dma_start(w_qkv[:, r, :], io[f"L0_gnn_{x}w"]).then_inc(weights_in, 16)
                        sp.dma_start(b_qkv[r][:, :], row_vector(f"L0_gnn_{x}b")).then_inc(weights_in, 16)
                    sp.wait_ge(step, 1)
                    sp.dma_start(dst_rows.rearrange("(p c) e -> p (c e)", c=4), rows_f[:, :, :].rearrange("p c e -> p (c e)")).then_inc(rows_out, 16)
                    sp.wait_ge(step, 5)
                    for d in range(2):
                        sp.dma_start(dst_digits[d, :].rearrange("(p e) -> p e", p=TAB_P), digit_b[:, d, :]).then_inc(digits_out, 16)
                    sp.wait_ge(step, 20)
                    sp.dma_start(ranges_d.rearrange("(p c) -> p c", c=4), word[:, :]).then_inc(ranges_out, 16)
                    sp.wait_ge(ranges_out, 16)
                    sp.dma_start(ranges[:, :], ranges_d.rearrange("(a s) -> a s", a=1)).then_inc(ranges_in, 16)
                    sp.wait_ge(ea_cut, 3)
                    for part in range(3):
                        for w_part in range(3):
                            row = ED * (3 * part + w_part)
                            sp.dma_start(ea_parts[row:row + ED, :].rearrange("c (q e) -> (c q) e", q=EA_SPLIT), ea_b[:, part, :]).then_inc(ea_out, 16)
                    sp.wait_ge(w_split, 10)
                    for n in range(2):
                        sp.dma_start(w_parts_d[n, :, :].rearrange("(p c) d -> c p d", c=ED), w_edge_b[:, n, :, :]).then_inc(w_out, 16)
                    sp.wait_ge(w_out, 32)
                    for n in range(2):
                        for part in range(3):
                            sp.dma_start(w_edge[n][3 * ED * part:3 * ED * (part + 1), :], w_parts_d[n, :, :]).then_inc(w_edge_in, 16)
                    sp.wait_ge(rows_out, 16)
                    sp.wait_ge(digits_out, 32)
                    sp.wait_ge(ranges_in, 16)
                    sp.wait_ge(ea_out, 144)
                    sp.wait_ge(w_edge_in, 96)

                @block.scalar
                def _(act):
                    act.wait_ge(ea_in, 16)
                    act.activation(ea_b[:, 0, :], ea_f, ACT.Copy).then_inc(ea_cut, 1)
                    for part in range(1, 3):
                        act.wait_ge(ea_left, part)
                        act.activation(ea_b[:, part, :], ea_f, ACT.Copy).then_inc(ea_cut, 1)

                @block.vector
                def _(dve):
                    count = [0]

                    def done(ins):
                        count[0] += 1
                        ins.then_inc(step, 1)
                        dve.wait_ge(step, count[0])

                    dve.wait_ge(dst_in, 32)
                    done(dve.tensor_copy(rows_f[:, :, :].rearrange("p c e -> p (c e)"), rows_i[:, :]))
                    done(dve.tensor_scalar(digit_i[:, 0, :], rows_i[:, :], 7, None, ALU.arith_shift_right))
                    done(dve.tensor_scalar(digit_i[:, 1, :], rows_i[:, :], P - 1, None, ALU.bitwise_and))
                    done(dve.tensor_copy(digit_b[:, 0, :], digit_i[:, 0, :]))
                    done(dve.tensor_copy(digit_b[:, 1, :], digit_i[:, 1, :]))
                    done(dve.tensor_reduce(ends_f[:, :, 0], rows_f[:, :, :], AX.X, ALU.min))
                    done(dve.tensor_reduce(ends_f[:, :, 1], rows_f[:, :, :], AX.X, ALU.max))
                    done(dve.tensor_copy(ends_i[:, :, :], ends_f[:, :, :]))
                    done(dve.tensor_scalar(range_i[:, :, 0:2], ends_i[:, :, :], 7, None, ALU.arith_shift_right))
                    done(dve.tensor_scalar(range_i[:, :, 2:4], ends_i[:, :, :], 4, None, ALU.arith_shift_right))
                    done(dve.tensor_copy(range_f[:, :, :], range_i[:, :, :]))
                    ends = range_f[:, :, :].rearrange("p c (t e) -> p (c t) e", e=2)[:, :, 1]
                    done(dve.tensor_scalar(ends, ends, 1.0, None, ALU.add))
                    done(dve.tensor_copy(range_o[:, :, :], range_f[:, :, :]))
                    for n in range(1, 4):
                        done(dve.tensor_scalar(range_o[:, :, n], range_o[:, :, n], RANGE_AT[n], None, ALU.logical_shift_left))
                        done(dve.tensor_tensor(range_o[:, :, 0], range_o[:, :, 0], range_o[:, :, n], ALU.bitwise_or))
                    done(dve.tensor_copy(word[:, :], range_o[:, :, 0]))
                    done(dve.tensor_copy(dst_cols[:, :], cols_i[:, :]))
                    dve.wait_ge(iota_done, 5)
                    done(dve.tensor_copy(pid_f[:, :], pid_i[:, :]))
                    done(dve.tensor_copy(iota_row[:, :], iota_i[:, :]))
                    done(dve.tensor_scalar(ident[:, :], iota_row[:, :], pid_f[:, 0:1], None, ALU.is_equal))
                    done(dve.tensor_copy(ident_b[:, :], ident[:, :]))
                    for part in range(1, 3):
                        dve.wait_ge(ea_cut, part)
                        dve.tensor_tensor(ea_f, ea_f, ea_b[:, part - 1, :], ALU.subtract).then_inc(ea_left, 1)
                    done(dve.tensor_copy(node_of[:, :], node_i[:, :]))
                    done(dve.tensor_copy(neg_block[:, :], negb_i[:, :]))
                    done(dve.tensor_copy(win_node[:, :], win_i[:, :]))
                    done(dve.tensor_scalar(lane_i[:, :], pid_i[:, :], WIN - 1, None, ALU.bitwise_and))
                    done(dve.tensor_copy(lane_f[:, :], lane_i[:, :]))
                    done(dve.tensor_scalar(win_node[:, :], win_node[:, :], lane_f[:, 0:1], None, ALU.add))
                    done(dve.tensor_scalar(digit_w[:, :], iota_row[0:2, :], 0.0, 1.0, ALU.mult, ALU.add))
                    done(dve.memset(digit_w[0:1, :], float(P)))
                    done(dve.tensor_scalar(neg_node[:, :], node_of[:, :], -1.0, None, ALU.mult))
                    done(dve.tensor_scalar(neg_win[:, :], win_node[:, :], -PEN, None, ALU.mult))
                    done(dve.memset(one_col[:, :], 1.0))
                    done(dve.memset(eps_col[:, :], EPS))
                    dve.wait_ge(weights_in, 224)
                    for n in range(2):
                        for r, rows in ((0, P), (1, P), (2, ED), (3, P)):
                            w = w_raw[0:rows, 4 * n + r, :].rearrange("p (g c) -> p g c", c=GC)
                            mean = w_mean[0:rows, 4 * n + r, :]
                            to = (w_pair[n][:, 0, :], w_pair[n][:, 1, :], w_edge_f[:, n, :], b1_row[n][:, :])[r]
                            done(dve.tensor_reduce(mean, w, AX.X, ALU.add))
                            done(dve.tensor_scalar(mean, mean, -1.0 / GC, None, ALU.mult))
                            done(dve.tensor_tensor(to.rearrange("p (g c) -> p g c", c=GC), w,
                                                   mean.unsqueeze(2).to_broadcast([rows, GROUPS, GC]), ALU.add))
                    split = chain(dve, w_split, 0)
                    for n in range(2):
                        split_parts(dve, split, w_edge_f[:, n, :], [w_edge_b[:, n, part, :] for part in range(3)])

        with ExitStack() as st:
            def b(name, shape, dt=F32):
                return st.enter_context(nc.sbuf_tensor(f"ln_{name}", shape, dt))

            xc, sq, stat = b("x", [P, CHUNK, D]), b("sq", [P, CHUNK, D]), b("stat", [P, 4, CHUNK])
            x_in, x_free, step, sq_done, std_done, kept, paced = (
                sem(f"ln_{n}") for n in ("x_in", "x_free", "step", "sq", "std", "kept", "paced"))
            K = 7
            with nc.Block() as block:
                @block.sync
                def _(sp):
                    with sp.Fori(0, CHUNKS) as i:
                        sp.wait_ge(x_free, i + 1)
                        sp.dma_start(xc[:, :, :], by_block(io["x_rows"], i)).then_inc(x_in, 16)
                        hold(sp, step, K * (i + 1), paced)
                        sp.dma_start(by_block(resid, i), hidden[:, bass.ds(CHUNK * i, CHUNK), :]).then_inc(kept, 16)
                    sp.wait_ge(kept, 16 * CHUNKS)

                @block.vector
                def _(dve):
                    dve.sem_inc(x_free, 1)
                    with dve.Fori(0, CHUNKS) as i:
                        done = chain(dve, step, K * i)
                        wide = lambda v: v.unsqueeze(2).to_broadcast([P, CHUNK, D])
                        h = hidden[:, bass.ds(CHUNK * i, CHUNK), :]
                        dve.wait_ge(x_in, 16 * (i + 1))
                        done(dve.tensor_reduce(stat[:, 0, :], xc[:, :, :], AX.X, ALU.add))
                        done(dve.tensor_scalar(stat[:, 0, :], stat[:, 0, :], -1.0 / D, None, ALU.mult))
                        done(dve.tensor_tensor(xc[:, :, :], xc[:, :, :], wide(stat[:, 0, :]), ALU.add))
                        dve.wait_ge(sq_done, i + 1)
                        done(dve.tensor_reduce(stat[:, 1, :], sq[:, :, :], AX.X, ALU.add))
                        dve.wait_ge(std_done, i + 1)
                        done(dve.reciprocal(stat[:, 3, :], stat[:, 2, :]))
                        done(dve.tensor_tensor(xc[:, :, :], xc[:, :, :], wide(stat[:, 3, :]), ALU.mult))
                        done(dve.tensor_scalar(h, xc[:, :, :], 0.0, None, ALU.max))
                        dve.sem_inc(x_free, 1)

                @block.scalar
                def _(act):
                    with act.Fori(0, CHUNKS) as i:
                        act.wait_ge(step, K * i + 3)
                        act.activation(sq[:, :, :], xc[:, :, :], ACT.Square).then_inc(sq_done, 1)
                        act.wait_ge(step, K * i + 4)
                        act.activation(stat[:, 2, :], stat[:, 1, :], ACT.Sqrt, bias=eps_col[:, 0:1],
                                       scale=1.0 / D).then_inc(std_done, 1)

        def project(tag, weights, biases, table):
            n = len(weights)
            in_parts = n == 2
            with ExitStack() as st:
                def b(name, shape, dt=F32):
                    return st.enter_context(nc.sbuf_tensor(f"{tag}_{name}", shape, dt))

                stage, hT, rest = b("stage", [P, CHUNK, D]), b("hT", [P, CC]), b("rest", [P, CHUNK, D])
                outs = b("outs", [P, CHUNK, 3 * D], BF16) if in_parts else b("outs", [P, CHUNK, (n - 1) * D])
                staged, hT_ps, hT_done, out_done, stored, step, rest_done = (
                    sem(f"{tag}_{x}") for x in ("staged", "hT_ps", "hT", "out", "stored", "step", "rest"))
                part_ps = [sem(f"{tag}_part_ps{r}") for r in range(n)]
                part_free = [sem(f"{tag}_part_free{r}") for r in range(n)]
                trans = banks(0, CC)
                parts = [banks(2 + 2 * r, CC).rearrange("p (k c) -> p k c", c=D) for r in range(n)]
                with nc.Block() as block:
                    @block.scalar
                    def _(act):
                        act.sem_inc(hT_done, 1)
                        with act.Fori(0, CHUNKS) as i:
                            act.activation(stage[:, :, :], hidden[:, bass.ds(CHUNK * i, CHUNK), :],
                                           ACT.Copy).then_inc(staged, 1)
                            act.wait_ge(hT_ps, i + 1)
                            act.activation(hT[:, :], trans, ACT.Copy).then_inc(hT_done, 1)
                            act.wait_ge(part_ps[n - 1], i + 1)

                    @block.tensor
                    def _(pe):
                        with pe.Fori(0, CHUNKS) as i:
                            pe.wait_ge(staged, i + 1)
                            pe.wait_ge(hT_done, i + 1)
                            for k in range(CHUNK):
                                last = pe.transpose(trans[:, k * D:(k + 1) * D], stage[:, k, :], ident[:, :])
                            last.then_inc(hT_ps, 1)
                            pe.wait_ge(hT_done, i + 2)
                            for r in range(n):
                                pe.wait_ge(part_free[r], i + 1)
                                for k in range(CHUNK):
                                    last = pe.matmul(parts[r][:, k, :], hT[:, k * D:(k + 1) * D], weights[r],
                                                     start=True, stop=True)
                                last.then_inc(part_ps[r], 1)

                    STEPS = 12 if in_parts else 6

                    @block.vector
                    def _(dve):
                        for r in range(n):
                            dve.sem_inc(part_free[r], 1)
                        with dve.Fori(0, CHUNKS) as i:
                            done = chain(dve, step, STEPS * i)
                            dst = [dst_parts[:, bass.ds(CHUNK * i, CHUNK), p, :] for p in range(3)]
                            dve.wait_ge(part_ps[0], i + 1)
                            done(dve.tensor_tensor(rest[:, :, :], parts[0], row_of(biases[0]), ALU.add))
                            dve.sem_inc(part_free[0], 1)
                            split_parts(dve, done, rest[:, :, :], dst)
                            dve.wait_ge(stored, 16 * i + 16)
                            if in_parts:
                                dve.wait_ge(part_ps[1], i + 1)
                                done(dve.tensor_copy(rest[:, :, :], parts[1]))
                                dve.sem_inc(part_free[1], 1)
                                split_parts(dve, done, rest[:, :, :], [outs[:, :, p * D:(p + 1) * D] for p in range(3)])
                                dve.sem_inc(out_done, 1)
                            else:
                                for r in range(1, n):
                                    dve.wait_ge(part_ps[r], i + 1)
                                    dve.tensor_tensor(outs[:, :, (r - 1) * D:r * D], parts[r], row_of(biases[r]),
                                                      ALU.add).then_inc(part_free[r], 1)
                                    dve.wait_ge(part_free[r], i + 2)
                                dve.sem_inc(out_done, 1)

                    @block.sync
                    def _(sp):
                        sp.sem_inc(stored, 16)
                        with sp.Fori(0, CHUNKS) as i:
                            sp.wait_ge(out_done, i + 1)
                            sp.dma_start(by_block(table, i), outs[:, :, :]).then_inc(stored, 16)
                        sp.wait_ge(stored, 16 * (CHUNKS + 1))

        ENGINES = {"pe": mybir.EngineType.PE, "act": mybir.EngineType.Activation, "dve": mybir.EngineType.DVE}

        def span(eng, s):
            word = nc.values_load(ranges[0:1, bass.ds(s, 1)], engines=(ENGINES[eng],), min_val=0, max_val=2 ** 30 - 1,
                                  skip_runtime_bounds_check_because="made on the chip of dst, which lies in the nodes")
            part = lambda n, low, high: ((word >> RANGE_AT[n]) & (2 ** RANGE_BITS[n] - 1)).with_bounds(min_val=low, max_val=high)
            return ((part(0, 0, BLOCKS - 1), part(1, 1, BLOCKS)), (part(2, 0, WINDOWS - 1), part(3, 1, WINDOWS)))

        def span_registers(eng, tag):
            return [[eng.alloc_register(f"{tag}_{end}{r}") for end in ("first", "end")] for r in range(DEPTH)]

        def keep_span(eng, kept, ends):
            for reg, end in zip(kept, ends):
                eng.reg_mov(reg, end)
            return kept_span(eng, kept)

        def kept_span(eng, kept):
            return value(eng, kept[0], 0, BLOCKS - 1), value(eng, kept[1], 1, BLOCKS)

        def pairs(eng, ends, body, step=1):
            with eng.Fori(*ends, step) as n:
                body(n)

        def counter(eng, name, start):
            reg = eng.alloc_register(name)
            eng.reg_mov(reg, start)
            return reg

        def value(eng, reg, low, high=BLOCKS * SUPERS + 8):
            return eng.snap(reg, min_val=low, max_val=high)

        def edge_sems(tag, names, loads):
            t = {x: sem(f"{tag}_{x}") for x in names}
            t.update({x: [sem(f"{tag}_{x}{r}") for r in range(DEPTH)] for x in loads})
            return t

        def pick_act(act, S, reg, side, ends, dst_ps, apart, pick, ready):
            def body(blk):
                q = value(act, reg, 1)
                act.wait_ge(*ready)
                hold(act, S["pick"], q, S["act_paced"])
                act.activation(apart[:, :], dst_ps, ACT.Square,
                               bias=neg_node[:, bass.ds(blk, 1)]).then_inc(S["apart"], 1)
                act.wait_ge(S["pick_free"], q)
                hold(act, S["apart"], q, S["act_paced"])
                to = pick[:, 0, :] if side is None else pick[:, bass.ds(value(act, side, 0, 1), 1), :].rearrange("p a e -> p (a e)")
                act.activation(to, apart[:, :], ACT.Relu, bias=one_col[:, 0:1], scale=-1.0).then_inc(S["pick"], 1)
                if side is not None:
                    act.reg_sub(side, 1, side)
                act.reg_add(reg, reg, 1)
            pairs(act, ends, body)

        def pick_pe(pe, S, reg, side, ends, to, pick, rows):
            def body(blk):
                q = value(pe, reg, 1)
                half = 0 if side is None else bass.ds(value(pe, side, 0, 1), 1)
                table = rows(blk)
                pe.wait_ge(S["pick"], q + 1)
                for j in range(TILES):
                    for part in table:
                        names = pick[:, half, j * P:(j + 1) * P]
                        last = pe.matmul(to[:, j, :], names if side is None else names.rearrange("p a e -> p (a e)"),
                                         part, start=False, stop=False, skip_group_check=True)
                last.then_inc(S["pick_free"], 1)
                if side is not None:
                    pe.reg_sub(side, 1, side)
                pe.reg_add(reg, reg, 1)
            pairs(pe, ends, body)

        def parts_of_dst(blk):
            return [dst_parts[:, bass.ds(blk, 1), part, :].rearrange("p a c -> p (a c)") for part in range(3)]

        def scatter_dve(dve, S, reg, before, ends, s, node_row, hot, width):
            def body(blk):
                q = value(dve, reg, 1)
                dve.wait_ge(S["sums"], q)
                dve.tensor_tensor(hot[:, :, :], node_row[:, bass.ds(blk, 1), :].to_broadcast([P, TILES, P]),
                                  dst_cols[:, bass.ds(TILES * s, TILES)].unsqueeze(2).to_broadcast([P, TILES, P]),
                                  ALU.is_equal).then_inc(S["hot"], 1)
                add_sums(dve, S, q, before, width)
                dve.reg_mov(before, blk)
                dve.reg_add(reg, reg, 1)
            pairs(dve, ends, body)

        def number_nodes(pool, dve, node_row, made):
            if pool:
                pool.iota(node_row[:, :, :].bitcast(I32), [[P, BLOCKS], [1, P]], base=0, channel_multiplier=0).then_inc(made, 1)
            if dve:
                dve.wait_ge(made, 1)
                dve.tensor_copy(node_row[:, :, :], node_row[:, :, :].bitcast(I32)).then_inc(made, 1)
                dve.wait_ge(made, 2)

        def add_sums(dve, S, q, before, width):
            dve.wait_ge(S["sums_free"], q)
            to = acc[:, bass.ds(value(dve, before, 0, BLOCKS - 1), 1), 0:width].rearrange("p a c -> p (a c)")
            dve.tensor_tensor(to, bank(SUMS)[:, 0:width], to, ALU.add).then_inc(S["sums_free"], 1)

        def scatter_pe(pe, S, reg, ends, hot, vals, width, ready):
            def body(blk):
                q = value(pe, reg, 1)
                pe.wait_ge(*ready)
                pe.wait_ge(S["hot"], q)
                pe.wait_ge(S["sums_free"], q + 1)
                for j in range(TILES):
                    last = pe.matmul(bank(SUMS)[:, 0:width], hot[:, j, :], vals[:, j, 0:width],
                                     start=(j == 0), stop=(j == TILES - 1))
                last.then_inc(S["sums"], 1)
                pe.reg_add(reg, reg, 1)
            pairs(pe, ends, body)
            pe.matmul(bank(SPARE)[:, 0:1], ident[:, :], ident[:, 0:1], start=True, stop=True).then_inc(S["vals_free"], 1)

        SUMS, SPARE = 6, 7

        def conv(tag, layer):
            with ExitStack() as st:
                def b(name, shape, dt=F32):
                    return st.enter_context(nc.sbuf_tensor(f"{tag}_{name}", shape, dt))

                def b2(name, shape, dt=F32):
                    return [b(f"{name}{g}", shape, dt) for g in range(2)]

                def deep(name, shape, dt=F32):
                    return [b(f"{name}{r}", shape, dt) for r in range(DEPTH)]

                idx, dst, ea = deep("idx", [P, TILES], I32), deep("dst", [P, SUPER]), deep("ea", [9 * ED, SUPER], BF16)
                rows = deep("rows", [P, TILES, 3 * D], BF16)
                apart, pick = b("apart", [P, SUPER]), b("pick", [P, 2, SUPER], BF16)
                sq = b2("sq", [P, TILES * D])
                var, root_t, root_p = (b(x, [P, 2, TILES * GROUPS]) for x in ("var", "root_t", "root_p"))
                rstd = b2("rstd", [P, 2, TILES * GROUPS])
                y, vals = b2("y", [P, TILES, D]), b2("vals", [P, TILES, D + 1])
                hot, node_row = b("hot", [P, TILES, P]), b("node_row", [P, BLOCKS, P])
                gamma, beta = b("gamma", [P, D]), b("beta", [P, D])
                S = edge_sems(tag, ("affine_in", "nodes", "apart", "pick", "pick_free", "hot", "sums", "sums_free", "ones",
                                    "sp_paced", "pool_paced", "act_paced", "pe_paced", "picked", "rows_free", "message",
                                    "sq", "ssq", "root", "scaled", "gained", "y", "vals", "vals_free"),
                              ("idx_in", "dst_in", "ea_in", "rows_in"))
                MSG = (0, 1, 2, 3)
                MESSAGE, SQUARE, VARIANCE, SCALE, SILU, SCATTER = 1, 2, 2, 4, 5, 5
                grouped = [TILES * GROUPS, GC]
                with nc.Block() as block:
                    @block.sync
                    def _(sp):
                        sp.dma_start(gamma[:, :], row_vector(f"L0_gnn_c{layer + 1}_g")).then_inc(S["affine_in"], 16)
                        sp.dma_start(beta[:, :], row_vector(f"L0_gnn_c{layer + 1}_bt")).then_inc(S["affine_in"], 16)

                        def body(stage):
                            s, r, k = stage(0)
                            hold(sp, S["rows_in"][r], 16 * TILES * k, S["sp_paced"])
                            sp.dma_start(idx[r][:, :], io["src_idx"][bass.ds(s, 1), :, :].rearrange("a p j -> (a p) j")).then_inc(S["idx_in"][r], 16)
                            hold(sp, S["picked"], s - (DEPTH - 1), S["sp_paced"])
                            sp.dma_start(dst[r][:, :], dst_rows[bass.ds(s, 1), :].to_broadcast([P, SUPER])).then_inc(S["dst_in"][r], 16)
                            hold(sp, S["message"], s - (DEPTH - 1), S["sp_paced"])
                            sp.dma_start(ea[r][:, :], ea_parts[:, bass.ds(s * SUPER, SUPER)]).then_inc(S["ea_in"][r], 16)
                        slots(sp, 0, body)

                    @block.gpsimd
                    def _(pool):
                        number_nodes(pool, None, node_row, S["nodes"])

                        def body(stage):
                            s, r, k = stage(0)
                            hold(pool, S["idx_in"][r], 16 * (k + 1), S["pool_paced"])
                            hold(pool, S["rows_free"], s - (DEPTH - 1), S["pool_paced"])
                            for j in range(TILES):
                                pool.indirect_dma_start(
                                    rows[r][:, j, :], None, src_table,
                                    bass.IndirectOffsetOnAxis(idx[r][:, j:j + 1], 0)).then_inc(S["rows_in"][r], 16)
                        slots(pool, 0, body)

                    @block.tensor
                    def _(pe):
                        picked, scattered = counter(pe, f"{tag}_picked", 1), counter(pe, f"{tag}_scattered", 1)
                        side = counter(pe, f"{tag}_side", 0)
                        kept = span_registers(pe, tag)
                        pe.wait_ge(S["ones"], 1)
                        pe.matmul(bank(SUMS)[:, 0:D + 1], hot[:, 0, :], vals[0][:, 0, :], start=True, stop=True).then_inc(S["sums"], 1)

                        def body(stage):
                            far = stage(SCATTER) and kept_span(pe, kept[stage(SCATTER)[1]])
                            near = stage(MESSAGE) and keep_span(pe, kept[stage(MESSAGE)[1]], span("pe", stage(MESSAGE)[0])[0])
                            if stage(MESSAGE):
                                s, r, k = stage(MESSAGE)
                                pe.wait_ge(S["rows_in"][r], 16 * TILES * (k + 1))
                                wait(pe, S["scaled"], s - (DEPTH - 1))
                                for p in range(3):
                                    last = pe.matmul(bank(MSG[r]).rearrange("p (j c) -> p j c", c=D), ident_b[:, :], rows[r][:, :, p * D:(p + 1) * D],
                                                     start=(p == 0), stop=False, skip_group_check=True)
                                last.then_inc(S["rows_free"], 1)
                                pe.wait_ge(S["ea_in"][r], 16 * (k + 1))

                                def edge_part(j):
                                    return pe.matmul(bank(MSG[r])[:, j * D:(j + 1) * D], ea[r][:, j * P:(j + 1) * P],
                                                     w_edge[layer][:, :], start=False, stop=(j == TILES - 1), skip_group_check=True)

                                for j in range(TILES - 1):
                                    edge_part(j)
                                pick_pe(pe, S, picked, side, near, bank(MSG[r]).rearrange("p (j c) -> p j c", c=D), pick, parts_of_dst)
                                edge_part(TILES - 1).then_inc(S["message"], 1)
                            if stage(SCATTER):
                                s, r, k = stage(SCATTER)
                                scatter_pe(pe, S, scattered, far, hot, vals[r % 2], D + 1, (S["vals"], s + 1))
                        slots(pe, SCATTER, body)

                    @block.scalar
                    def _(act):
                        picked = counter(act, f"{tag}_picked", 1)
                        side = counter(act, f"{tag}_side", 0)
                        act.sem_inc(S["pick"], 1)

                        def body(stage):
                            ends = stage(0) and span("act", stage(0)[0])[0]
                            if stage(SQUARE):
                                s, r, k = stage(SQUARE)
                                act.wait_ge(S["message"], s + 1)
                                wait(act, S["ssq"], s - 1)
                                act.activation(sq[r % 2][:, :], bank(MSG[r]), ACT.Square, scale=GC ** -0.5).then_inc(S["sq"], 1)
                            if stage(SILU):
                                s, r, k = stage(SILU)
                                act.wait_ge(S["y"], s + 1)
                                wait(act, S["vals_free"], s - 1)
                                act.activation(vals[r % 2][:, :, 0:D], y[r % 2][:, :, :], ACT.Silu).then_inc(S["vals"], 1)
                            if stage(0):
                                s, r, k = stage(0)
                                pick_act(act, S, picked, side, ends, dst[r][:, :], apart, pick, (S["dst_in"][r], 16 * (k + 1)))
                                act.sem_inc(S["picked"], 1)
                        slots(act, SILU, body)

                    @block.vector
                    def _(dve):
                        scattered, before = counter(dve, f"{tag}_scattered", 1), counter(dve, f"{tag}_before", 0)
                        dve.sem_inc(S["pick_free"], 2)
                        number_nodes(None, dve, node_row, S["nodes"])
                        for g in range(2):
                            dve.memset(vals[g][:, :, :], 0.0)
                        dve.memset(hot[:, :, :], 0.0)
                        dve.memset(acc[:, :, :], 0.0).then_inc(S["sums_free"], 1)
                        dve.wait_ge(S["sums_free"], 1)
                        dve.memset(vals[1][:, :, D:D + 1], 1.0)
                        dve.memset(vals[0][:, :, D:D + 1], 1.0).then_inc(S["ones"], 1)
                        dve.wait_ge(S["affine_in"], 32)
                        dve.tensor_scalar(gamma[:, :], gamma[:, :], ROOT_K, None, ALU.mult).then_inc(S["affine_in"], 1)
                        dve.wait_ge(S["affine_in"], 33)

                        def body(stage):
                            if stage(VARIANCE):
                                s, r, k = stage(VARIANCE)
                                dve.wait_ge(S["sq"], s + 1)
                                dve.tensor_reduce(var[:, r % 2, :], sq[r % 2][:, :].rearrange("p (a c) -> p a c", c=GC), AX.X, ALU.add).then_inc(S["ssq"], 1)
                            steps = []
                            if stage(VARIANCE) and stage(VARIANCE)[1] % 2:
                                s, r, k = stage(VARIANCE)
                                dve.wait_ge(S["ssq"], s + 1)
                                steps = list(root_steps(dve, *(x[:, :, :].rearrange("p g c -> p (g c)") for x in (var, rstd[r // 2], root_t, root_p))))
                                base = ROOT_STEPS * (DEPTH // 2 * k + r // 2)

                            def root_step():
                                if steps:
                                    n = ROOT_STEPS - len(steps)
                                    if n:
                                        dve.wait_ge(S["root"], base + n)
                                    steps.pop(0)().then_inc(S["root"], 1)

                            root_step()
                            if stage(SCALE):
                                s, r, k = stage(SCALE)
                                wait(dve, S["root"], ROOT_STEPS * (DEPTH // 2 * k + r // 2 + 1))
                                wait(dve, S["vals"], s - 1)
                                dve.tensor_tensor(y[r % 2][:, :, :].rearrange("p j (a c) -> p (j a) c", c=GC),
                                                  bank(MSG[r]).rearrange("p (a c) -> p a c", c=GC),
                                                  rstd[r // 2][:, r % 2, :].unsqueeze(2).to_broadcast([P] + grouped), ALU.mult).then_inc(S["scaled"], 1)
                            root_step()
                            ends = stage(SCATTER) and span("dve", stage(SCATTER)[0])[0]
                            if stage(SCALE):
                                dve.wait_ge(S["scaled"], s + 1)
                                dve.tensor_tensor(y[r % 2][:, :, :], y[r % 2][:, :, :], gamma[:, :].unsqueeze(1).to_broadcast([P, TILES, D]),
                                                  ALU.mult).then_inc(S["gained"], 1)
                            root_step()
                            if stage(SCALE):
                                dve.wait_ge(S["gained"], s + 1)
                                dve.tensor_tensor(y[r % 2][:, :, :], y[r % 2][:, :, :], beta[:, :].unsqueeze(1).to_broadcast([P, TILES, D]),
                                                  ALU.add).then_inc(S["y"], 1)
                            root_step()
                            if stage(SCATTER):
                                s, r, k = stage(SCATTER)
                                scatter_dve(dve, S, scattered, before, ends, s, node_row, hot, D + 1)
                            while steps:
                                root_step()
                        slots(dve, SCATTER, body)
                        q = value(dve, scattered, 1)
                        dve.wait_ge(S["sums"], q)
                        add_sums(dve, S, q, before, D + 1)

        def time_vector(tvec):
            with ExitStack() as st:
                def b(name, shape, dt=F32):
                    return st.enter_context(nc.sbuf_tensor(f"tv_{name}", shape, dt))

                n = TD // P
                emb, gate, spread = b("emb", [P, n]), b("gate", [P, n]), b("spread", [P, n, P])
                w, bias = b("w", [P, n, D]), b("bias", [P, D])
                loaded, gated, spread_done, product, vec_done = (
                    sem(f"tv_{x}") for x in ("loaded", "gated", "spread", "product", "vec"))
                with nc.Block() as block:
                    @block.sync
                    def _(sp):
                        sp.dma_start(emb[:, :], io["L0_gnn_t_emb"].rearrange("(p a) -> p a", a=n)).then_inc(loaded, 16)
                        sp.dma_start(w[:, :, :], io["L0_gnn_tm_w"].rearrange("(p a) c -> p a c", a=n)).then_inc(loaded, 16)
                        sp.dma_start(bias[:, :], row_vector("L0_gnn_tm_b")).then_inc(loaded, 16)

                    @block.scalar
                    def _(act):
                        act.wait_ge(loaded, 48)
                        act.activation(gate[:, :], emb[:, :], ACT.Silu).then_inc(gated, 1)

                    @block.vector
                    def _(dve):
                        dve.wait_ge(gated, 1)
                        dve.tensor_copy(spread[:, :, :], gate[:, :].unsqueeze(2).to_broadcast([P, n, P])).then_inc(spread_done, 1)
                        dve.wait_ge(product, 1)
                        dve.tensor_tensor(tvec[:, :], bank(0)[:, 0:D], bias[:, :], ALU.add).then_inc(vec_done, 1)

                    @block.tensor
                    def _(pe):
                        pe.wait_ge(spread_done, 1)
                        for a in range(n):
                            last = pe.matmul(bank(0)[:, 0:D], spread[:, a, :], w[:, a, :], start=(a == 0), stop=(a == n - 1))
                        last.then_inc(product, 1)

        def node_update(tag, weight, bias, gain, shift, then):
            attention = then == "out"
            STAGED = 3 if attention else 4
            CENTRED = STAGED + (1 if attention else 2)
            NORMED = CENTRED + 1 + ROOT_STEPS + 3
            STEPS = NORMED + (2 if attention else 1)
            with ExitStack() as st:
                def b(name, shape, dt=F32):
                    return st.enter_context(nc.sbuf_tensor(f"{tag}_{name}", shape, dt))

                w, bias_row, gain_row, shift_row = b("w", [P, D]), b("bias", [P, D]), b("gain", [P, D]), b("shift", [P, D])
                w_mean = b("w_mean", [P, 2, GROUPS])
                stage, hT, y, z, sq = (b(x, [P, CHUNK, D]) for x in ("stage", "hT", "y", "z", "sq"))
                extra = None if then == "time" else b("extra", [P, CHUNK, D])
                share, held = b("share", [P, CHUNK, HEADS]), b("held", [P, CHUNK, 1])
                var, rstd, root_t, root_p = (b(x, [P, CHUNK * GROUPS]) for x in ("var", "rstd", "root_t", "root_p"))
                loaded, ready, step, flipped, hT_done, product, squared, gated, x_in, stored = (
                    sem(f"{tag}_{x}") for x in ("loaded", "ready", "step", "flipped", "hT", "product", "squared", "gated", "x_in", "stored"))
                trans, prod = banks(0, CC), banks(2, CC).rearrange("p (k c) -> p k c", c=D)
                flat = lambda t: t[:, :, :].rearrange("p k c -> p (k c)")
                grouped = lambda t: t.rearrange("p k (g c) -> p (k g) c", c=GC)
                with nc.Block() as block:
                    @block.sync
                    def _(sp):
                        sp.dma_start(w[:, :], io[weight]).then_inc(loaded, 16)
                        for row, name in ((bias_row, bias), (gain_row, gain), (shift_row, shift)):
                            sp.dma_start(row[:, :], row_vector(name)).then_inc(loaded, 16)
                        if then == "residual":
                            with sp.Fori(0, CHUNKS) as i:
                                sp.wait_ge(step, STEPS * i + 1)
                                sp.dma_start(extra[:, :, :], by_block(resid, i)).then_inc(x_in, 16)
                        if attention:
                            sp.sem_inc(stored, 16)

                            def x_chunk(i):
                                sp.wait_ge(step, STEPS * i + 1)
                                sp.dma_start(extra[:, :, :], by_block(io["x_rows"], i)).then_inc(x_in, 16)
                                sp.wait_ge(step, STEPS * i + STEPS)

                            full = N_NODES // P
                            by_node = out[0:full * P, :].rearrange("(b p) c -> p b c", p=P)
                            with sp.Fori(0, CHUNKS - 1) as i:
                                x_chunk(i)
                                sp.dma_start(by_node[:, bass.ds(CHUNK * i, CHUNK), :], y[:, :, :]).then_inc(stored, 16)
                            x_chunk(CHUNKS - 1)
                            sp.dma_start(by_node[:, full - CHUNK + 1:full, :], y[:, 0:CHUNK - 1, :]).then_inc(stored, 16)
                            sp.dma_start(out[full * P:N_NODES, :], y[0:N_NODES - full * P, CHUNK - 1, :]).then_inc(stored, 16)
                            sp.wait_ge(stored, 16 * (CHUNKS + 2))

                    @block.vector
                    def _(dve):
                        setup = chain(dve, ready, 0)
                        dve.wait_ge(loaded, 64)
                        for n, t in enumerate((w, bias_row)):
                            groups = t[:, :].rearrange("p (g c) -> p g c", c=GC)
                            setup(dve.tensor_reduce(w_mean[:, n, :], groups, AX.X, ALU.add))
                            setup(dve.tensor_scalar(w_mean[:, n, :], w_mean[:, n, :], -1.0 / GC, None, ALU.mult))
                            setup(dve.tensor_tensor(groups, groups, w_mean[:, n, :].unsqueeze(2).to_broadcast([P, GROUPS, GC]), ALU.add))
                        setup(dve.tensor_scalar(gain_row[:, :], gain_row[:, :], ROOT_K, None, ALU.mult))
                        with dve.Fori(0, CHUNKS) as i:
                            done = chain(dve, step, STEPS * i)
                            blocks = bass.ds(CHUNK * i, CHUNK)
                            if attention:
                                done(dve.tensor_scalar(share[:, :, :], acc[:, blocks, D:D + HEADS], 1e-6, None, ALU.max))
                                done(dve.reciprocal(share[:, :, :], share[:, :, :]))
                                done(dve.tensor_tensor(stage[:, :, :].rearrange("p k (a c) -> p k a c", c=HD),
                                                       acc[:, blocks, 0:D].rearrange("p k (a c) -> p k a c", c=HD),
                                                       share[:, :, :].unsqueeze(3).to_broadcast([P, CHUNK, HEADS, HD]), ALU.mult))
                            else:
                                count = acc[:, blocks, D:D + 1]
                                done(dve.tensor_scalar(share[:, :, 0:1], count, 1.0, None, ALU.max))
                                done(dve.tensor_scalar(held[:, :, :], count, 1.0, None, ALU.min))
                                done(dve.reciprocal(share[:, :, 0:1], share[:, :, 0:1]))
                                done(dve.tensor_tensor(stage[:, :, :], acc[:, blocks, 0:D],
                                                       share[:, :, 0:1].to_broadcast([P, CHUNK, D]), ALU.mult))
                            if attention:
                                dve.wait_ge(stored, 16 * i + 16)
                                dve.wait_ge(product, i + 1)
                                done(dve.tensor_tensor(y[:, :, :], prod, row_of(bias_row), ALU.add))
                            else:
                                done(dve.tensor_tensor(y[:, :, :], row_of(bias_row), held[:, :, :].to_broadcast([P, CHUNK, D]), ALU.mult))
                                dve.wait_ge(product, i + 1)
                                done(dve.tensor_tensor(y[:, :, :], y[:, :, :], prod, ALU.add))
                            dve.wait_ge(squared, i + 1)
                            done(dve.tensor_reduce(var[:, :], grouped(sq[:, :, :]), AX.X, ALU.add))
                            for root_step in root_steps(dve, var[:, :], rstd[:, :], root_t[:, :], root_p[:, :]):
                                done(root_step())
                            done(dve.tensor_tensor(grouped(y[:, :, :]), grouped(y[:, :, :]),
                                                   rstd[:, :].unsqueeze(2).to_broadcast([P, CHUNK * GROUPS, GC]), ALU.mult))
                            done(dve.tensor_tensor(y[:, :, :], y[:, :, :], row_of(gain_row), ALU.mult))
                            done(dve.tensor_tensor(y[:, :, :], y[:, :, :], row_of(shift_row), ALU.add))
                            if then == "time":
                                dve.wait_ge(gated, i + 1)
                                done(dve.tensor_tensor(hidden[:, blocks, :], z[:, :, :], row_of(tvec), ALU.add))
                            elif then == "residual":
                                dve.wait_ge(x_in, 16 * (i + 1))
                                dve.wait_ge(gated, i + 1)
                                done(dve.tensor_tensor(hidden[:, blocks, :], z[:, :, :], extra[:, :, :], ALU.add))
                            else:
                                done(dve.tensor_tensor(y[:, :, :], y[:, :, :], hidden[:, blocks, :], ALU.add))
                                dve.wait_ge(x_in, 16 * (i + 1))
                                done(dve.tensor_tensor(y[:, :, :], y[:, :, :], extra[:, :, :], ALU.add))

                    @block.tensor
                    def _(pe):
                        pe.wait_ge(ready, 7)
                        with pe.Fori(0, CHUNKS) as i:
                            pe.wait_ge(step, STEPS * i + STAGED)
                            for k in range(CHUNK):
                                last = pe.transpose(trans[:, k * D:(k + 1) * D], stage[:, k, :], ident[:, :])
                            last.then_inc(flipped, 1)
                            pe.wait_ge(hT_done, i + 1)
                            for k in range(CHUNK):
                                last = pe.matmul(prod[:, k, :], hT[:, k, :], w[:, :], start=True, stop=True)
                            last.then_inc(product, 1)

                    @block.scalar
                    def _(act):
                        with act.Fori(0, CHUNKS) as i:
                            act.wait_ge(flipped, i + 1)
                            act.activation(flat(hT), trans, ACT.Copy).then_inc(hT_done, 1)
                            act.wait_ge(step, STEPS * i + CENTRED)
                            act.activation(sq[:, :, :], y[:, :, :], ACT.Square, scale=GC ** -0.5).then_inc(squared, 1)
                            if not attention:
                                act.wait_ge(step, STEPS * i + NORMED)
                                act.activation(z[:, :, :], y[:, :, :], ACT.Silu).then_inc(gated, 1)

        def logits_pass():
            with ExitStack() as st:
                def b(name, shape, dt=F32):
                    return st.enter_context(nc.sbuf_tensor(f"lg_{name}", shape, dt))

                def b2(name, shape, dt=F32):
                    return [b(f"{name}{g}", shape, dt) for g in range(2)]

                def deep(name, shape, dt=F32):
                    return [b(f"{name}{r}", shape, dt) for r in range(DEPTH)]

                idx, ea, digits = deep("idx", [P, TILES], I32), b2("ea", [ED + 1, SUPER]), deep("digits", [2, SUPER], BF16)
                rows = deep("rows", [P, TILES, 2 * D])
                pick, zeros = b("pick", [P, 2, SUPER], BF16), b("zeros", [2, SUPER], BF16)
                prod, dots = b("prod", [P, TILES, D]), b("dots", [P, TILES * HEADS])
                lg, lg_wide = b2("lg", [P, TILES * HEADS]), b2("lg_wide", [P, TILES, P])
                top, w_ea = b("top", [P, 2]), b("w_ea", [ED + 1, HEADS])
                spare = [acc[:, :, :].rearrange("p b c -> p (b c)")[:, n * SUPER:(n + 1) * SUPER] for n in range(DEPTH + 5)]
                dst, apart, masked, far = spare[:DEPTH], spare[DEPTH], spare[DEPTH + 1:DEPTH + 3], spare[DEPTH + 3:]
                S = edge_sems("lg", ("set", "weights", "apart", "pick", "pick_free", "picked", "sp_paced", "pool_paced", "act_paced",
                                     "dve_paced", "dst_again", "query", "prod", "dots", "logits", "wide", "kept", "spread",
                                     "far", "top", "top_kept", "windows", "topped"),
                              ("idx_in", "dst_in", "digits_in", "ea_in", "rows_in", "v_out"))
                QUERY, EDGE, AGAIN, WIDE = (0, 1), (2, 3), (4, 5), (6, 7)
                PROJECT, LOGIT, WIDEN, SPREAD, TOP = 1, 2, 3, 4, 5
                with nc.Block() as block:
                    @block.sync
                    def _(sp):
                        sp.dma_start(w_ea[0:ED, :], io["L0_gnn_ew"]).then_inc(S["weights"], 16)
                        sp.dma_start(w_ea[ED:ED + 1, :], io["L0_gnn_eb"].rearrange("(a n) -> a n", a=1)).then_inc(S["weights"], 16)
                        sp.wait_ge(S["set"], 1)

                        def body(stage):
                            if stage(0):
                                s, r, k = stage(0)
                                hold(sp, S["rows_in"][r], 16 * TILES * k, S["sp_paced"])
                                sp.dma_start(idx[r][:, :], io["src_idx"][bass.ds(s, 1), :, :].rearrange("a p j -> (a p) j")).then_inc(S["idx_in"][r], 16)
                                hold(sp, S["picked"], s - (DEPTH - 1), S["sp_paced"])
                                sp.dma_start(dst[r], dst_rows[bass.ds(s, 1), :].to_broadcast([P, SUPER])).then_inc(S["dst_in"][r], 16)
                            if stage(1):
                                s, r, k = stage(1)
                                hold(sp, S["rows_in"][r], 16 * TILES * (k + 1), S["sp_paced"])
                                sp.dma_start(v_edges[bass.ds(s, 1), :, :].rearrange("a p (j c) -> (a p) j c", c=D),
                                             rows[r][:, :, D:2 * D]).then_inc(S["v_out"][r], 16)
                            if stage(0):
                                s, r, k = stage(0)
                                hold(sp, S["query"], s - 1, S["sp_paced"])
                                sp.dma_start(ea[r % 2][0:ED, :], io["ea_rows"][:, bass.ds(s * SUPER, SUPER)]).then_inc(S["ea_in"][r], 16)
                            if stage(2):
                                s, r, k = stage(2)
                                hold(sp, S["dst_again"], s - (DEPTH - 1), S["sp_paced"])
                                sp.dma_start(digits[r][:, :], dst_digits[:, bass.ds(s * SUPER, SUPER)]).then_inc(S["digits_in"][r], 16)
                        slots(sp, 2, body)
                        for r in range(DEPTH):
                            sp.wait_ge(S["v_out"][r], 16 * ITERS)

                    @block.gpsimd
                    def _(pool):
                        def body(stage):
                            s, r, k = stage(0)
                            hold(pool, S["idx_in"][r], 16 * (k + 1), S["pool_paced"])
                            hold(pool, S["prod"], s - (DEPTH - 1), S["pool_paced"])
                            hold(pool, S["v_out"][r], 16 * k, S["pool_paced"])
                            for j in range(TILES):
                                pool.indirect_dma_start(
                                    rows[r][:, j, :], None, kv_table,
                                    bass.IndirectOffsetOnAxis(idx[r][:, j:j + 1], 0)).then_inc(S["rows_in"][r], 16)
                        slots(pool, 0, body)

                    @block.tensor
                    def _(pe):
                        picked, side = counter(pe, "lg_picked", 1), counter(pe, "lg_side", 0)
                        pe.wait_ge(S["weights"], 32)
                        pe.wait_ge(S["set"], 1)

                        def body(stage):
                            near = stage(PROJECT) and span("pe", stage(PROJECT)[0])[0]
                            if stage(SPREAD):
                                s, r, k = stage(SPREAD)
                                wait(pe, S["windows"], s - 1)
                                pe.wait_ge(S["digits_in"][r], 16 * (k + 1))
                                pe.matmul(bank(AGAIN[r % 2]), digit_w[:, :], digits[r][:, :], start=True, stop=True).then_inc(S["dst_again"], 1)
                                pe.wait_ge(S["wide"], s + 1)
                                wait(pe, S["topped"], s - 1)
                                for j in range(TILES):
                                    last = pe.matmul(bank(WIDE[r % 2])[:, j * P:(j + 1) * P], lg_wide[r % 2][:, j, :], ident[:, :],
                                                     start=(j == 0), stop=(j == TILES - 1), skip_group_check=True)
                                last.then_inc(S["spread"], 1)
                            if stage(PROJECT):
                                s, r, k = stage(PROJECT)
                                wait(pe, S["logits"], s - 1)
                                pe.matmul(bank(QUERY[r % 2]), digit_w[:, :], zeros[:, :], start=True, stop=False, skip_group_check=True)
                                pick_pe(pe, S, picked, side, near, bank(QUERY[r % 2]).rearrange("p (j c) -> p j c", c=D), pick, parts_of_dst)
                                pe.wait_ge(S["ea_in"][r], 16 * (k + 1))
                                for j in range(TILES):
                                    last = pe.matmul(bank(EDGE[r % 2])[:, j * HEADS:(j + 1) * HEADS], ea[r % 2][:, j * P:(j + 1) * P], w_ea[:, :],
                                                     start=(j == 0), stop=(j == TILES - 1), skip_group_check=True)
                                last.then_inc(S["query"], 1)
                        slots(pe, SPREAD, body)

                    @block.scalar
                    def _(act):
                        picked, side, seen = counter(act, "lg_picked", 1), counter(act, "lg_side", 0), counter(act, "lg_seen", 1)
                        act.sem_inc(S["pick"], 1)

                        def body(stage):
                            win_ends = stage(TOP) and span("act", stage(TOP)[0])[1]
                            if stage(TOP):
                                s, r, k = stage(TOP)

                                def couple(w):
                                    q = value(act, seen, 1, WINDOWS * SUPERS)
                                    act.wait_ge(S["dst_again"], s + 1)
                                    for h in range(2):
                                        hold(act, S["top"], 2 * q - 1 + h, S["act_paced"])
                                        act.activation(far[h], bank(AGAIN[r % 2]), ACT.Square, bias=neg_win[:, bass.ds(w + h, 1)], scale=PEN).then_inc(S["far"], 1)
                                    act.reg_add(seen, seen, 1)
                                pairs(act, win_ends, couple, 2)
                                act.wait_ge(S["far"], 2 * value(act, seen, 1, WINDOWS * SUPERS) - 2)
                                act.sem_inc(S["windows"], 1)
                            ends = stage(0) and span("act", stage(0)[0])[0]
                            if stage(WIDEN):
                                s, r, k = stage(WIDEN)
                                act.wait_ge(S["logits"], s + 1)
                                wait(act, S["spread"], s - 1)
                                act.activation(lg_wide[r % 2][:, :, :].rearrange("p j (h n) -> p (j h) n", n=WIN),
                                               lg[r % 2][:, :].unsqueeze(2).to_broadcast([P, TILES * HEADS, WIN]), ACT.Copy).then_inc(S["wide"], 1)
                                act.activation(logits[:, bass.ds(s, 1), :].rearrange("p a c -> p (a c)"), lg[r % 2][:, :], ACT.Copy).then_inc(S["kept"], 1)
                            if stage(0):
                                s, r, k = stage(0)
                                pick_act(act, S, picked, side, ends, dst[r], apart, pick, (S["dst_in"][r], 16 * (k + 1)))
                                act.sem_inc(S["picked"], 1)
                        slots(act, TOP, body)

                    @block.vector
                    def _(dve):
                        seen, before = counter(dve, "lg_seen", 1), counter(dve, "lg_before", 0)
                        dve.sem_inc(S["pick_free"], 2)
                        dve.sem_inc(S["top"], 2)
                        dve.sem_inc(S["top_kept"], 1)
                        dve.memset(top[:, :], NEG)
                        for g in range(2):
                            dve.memset(ea[g][:, :], 1.0)
                        dve.memset(zeros[:, :], 0.0)
                        dve.memset(tops[:, :], NEG).then_inc(S["set"], 1)
                        dve.wait_ge(S["set"], 1)

                        def keep_top(q):
                            dve.wait_ge(S["top"], 2 * q)
                            to = tops[:, bass.ds(value(dve, before, 0, WINDOWS - 1), 2)]
                            dve.tensor_tensor(to, to, top[:, :], ALU.max).then_inc(S["top_kept"], 1)

                        def body(stage):
                            if stage(LOGIT):
                                s, r, k = stage(LOGIT)
                                dve.wait_ge(S["query"], s + 1)
                                dve.wait_ge(S["rows_in"][r], 16 * TILES * (k + 1))
                                dve.tensor_tensor(prod[:, :, :], bank(QUERY[r % 2]).rearrange("p (j c) -> p j c", c=D),
                                                  rows[r][:, :, 0:D], ALU.mult).then_inc(S["prod"], 1)
                            if stage(TOP + 1):
                                dve.wait_ge(S["top"], 2 * value(dve, seen, 1, WINDOWS * SUPERS))
                                dve.sem_inc(S["topped"], 1)
                            win_ends = stage(TOP) and span("dve", stage(TOP)[0])[1]
                            if stage(LOGIT):
                                s, r, k = stage(LOGIT)
                                dve.wait_ge(S["prod"], s + 1)
                                dve.tensor_reduce(dots[:, :], prod[:, :, :].rearrange("p j (h c) -> p (j h) c", c=HD), AX.X, ALU.add).then_inc(S["dots"], 1)
                                dve.wait_ge(S["dots"], s + 1)
                                wait(dve, S["kept"], s - 1)
                                dve.scalar_tensor_tensor(lg[r % 2][:, :], dots[:, :], HD ** -0.5, bank(EDGE[r % 2])[:, 0:TILES * HEADS],
                                                         ALU.mult, ALU.add).then_inc(S["logits"], 1)
                            if stage(TOP):
                                s, r, k = stage(TOP)

                                def couple(w):
                                    q = value(dve, seen, 1, WINDOWS * SUPERS)
                                    keep_top(q)
                                    dve.wait_ge(S["spread"], s + 1)
                                    dve.wait_ge(S["top_kept"], q + 1)
                                    for h in range(2):
                                        hold(dve, S["far"], 2 * q - 1 + h, S["dve_paced"])
                                        dve.tensor_tensor_reduce(masked[h], bank(WIDE[r % 2]), far[h], 1.0, NEG,
                                                                 ALU.subtract, ALU.max, top[:, h:h + 1]).then_inc(S["top"], 1)
                                    dve.reg_mov(before, w)
                                    dve.reg_add(seen, seen, 1)
                                pairs(dve, win_ends, couple, 2)
                        slots(dve, TOP + 1, body)
                        keep_top(value(dve, seen, 1, WINDOWS * SUPERS))

        def node_maxima():
            with ExitStack() as st:
                quarter = WINDOWS // 4
                by_window = st.enter_context(nc.sbuf_tensor("by_window", [quarter, 4, WIN, HEADS], F32))
                by_block_ = st.enter_context(nc.sbuf_tensor("max_by_block", [P, BLOCKS, HEADS], F32))
                flipped, moved, written, loaded, step = (sem(f"max_{x}") for x in ("flipped", "moved", "written", "loaded", "step"))
                with nc.Block() as block:
                    @block.tensor
                    def _(pe):
                        for a in range(4):
                            last = pe.transpose(bank(0)[0:quarter, a * P:(a + 1) * P], tops[:, a * quarter:(a + 1) * quarter], ident[:, :])
                        last.then_inc(flipped, 1)

                    @block.sync
                    def _(sp):
                        sp.wait_ge(moved, 1)
                        sp.dma_start(max_nodes.rearrange("(a w n) h -> w a (n h)", a=4, n=WIN),
                                     by_window[:, :, :, :].rearrange("w a n h -> w a (n h)")).then_inc(written, 16)
                        sp.wait_ge(written, 16)
                        sp.dma_start(by_block_[:, :, :], max_nodes.rearrange("(b p) h -> p b h", p=P)).then_inc(loaded, 16)

                    @block.vector
                    def _(dve):
                        dve.wait_ge(flipped, 1)
                        for a in range(4):
                            last = dve.tensor_copy(by_window[:, a, :, :], bank(0)[0:quarter, a * P:(a + 1) * P].rearrange("w (h n) -> w n h", n=WIN))
                        last.then_inc(moved, 1)
                        dve.wait_ge(loaded, 16)
                        done = chain(dve, step, 0)
                        for p in range(3):
                            done(dve.tensor_copy(max_parts[:, :, p, :], by_block_[:, :, :]))
                            if p < 2:
                                done(dve.tensor_tensor(by_block_[:, :, :], by_block_[:, :, :], max_parts[:, :, p, :], ALU.subtract))

        def softmax_pass():
            with ExitStack() as st:
                def b(name, shape, dt=F32):
                    return st.enter_context(nc.sbuf_tensor(f"sm_{name}", shape, dt))

                def b2(name, shape, dt=F32):
                    return [b(f"{name}{g}", shape, dt) for g in range(2)]

                def deep(name, shape, dt=F32):
                    return [b(f"{name}{r}", shape, dt) for r in range(DEPTH)]

                dst, v = deep("dst", [P, SUPER]), deep("v", [P, TILES, D])
                apart, pick, zeros = b("apart", [P, SUPER]), b("pick", [P, 1, SUPER], BF16), b("zeros", [2, TILES * 3 * HEADS], BF16)
                below, top, vals = b2("below", [P, TILES * HEADS]), b2("top", [P, TILES * HEADS]), deep("vals", [P, TILES, ACC_W])
                hot = b("hot", [P, TILES, P])
                node_row = dst_parts[:, :, :, :].rearrange("p b k c -> p (b k c)")[:, 0:2 * NODES].bitcast(F32).rearrange("p (b n) -> p b n", n=P)
                S = edge_sems("sm", ("set", "nodes", "apart", "pick", "pick_free", "picked", "hot", "sums", "sums_free", "sp_paced",
                                     "act_paced", "maxima", "maxima_used", "below", "weight", "vals", "vals_free"), ("dst_in", "v_in"))
                MAX = (0, 1)
                MAXIMUM, BELOW, LOAD_V, EXPONENT, WEIGHT, SCATTER = 1, 2, 2, 3, 4, 5
                with nc.Block() as block:
                    @block.sync
                    def _(sp):
                        def body(stage):
                            if stage(0):
                                s, r, k = stage(0)
                                hold(sp, S["picked"], s - (DEPTH - 1), S["sp_paced"])
                                sp.dma_start(dst[r][:, :], dst_rows[bass.ds(s, 1), :].to_broadcast([P, SUPER])).then_inc(S["dst_in"][r], 16)
                            if stage(LOAD_V):
                                s, r, k = stage(LOAD_V)
                                hold(sp, S["vals"], s - (DEPTH - 1), S["sp_paced"])
                                sp.dma_start(v[r][:, :, :], v_edges[bass.ds(s, 1), :, :].rearrange("a p (j c) -> (a p) j c", c=D)).then_inc(S["v_in"][r], 16)
                        slots(sp, LOAD_V, body)

                    @block.gpsimd
                    def _(pool):
                        number_nodes(pool, None, node_row, S["nodes"])

                    @block.tensor
                    def _(pe):
                        picked, side, scattered = counter(pe, "sm_picked", 1), counter(pe, "sm_side", 0), counter(pe, "sm_scattered", 1)
                        kept = span_registers(pe, "sm")
                        pe.wait_ge(S["set"], 1)
                        pe.matmul(bank(SUMS)[:, 0:ACC_W], hot[:, 0, :], vals[0][:, 0, :], start=True, stop=True).then_inc(S["sums"], 1)

                        def body(stage):
                            far = stage(SCATTER) and kept_span(pe, kept[stage(SCATTER)[1]])
                            near = stage(MAXIMUM) and keep_span(pe, kept[stage(MAXIMUM)[1]], span("pe", stage(MAXIMUM)[0])[0])
                            if stage(MAXIMUM):
                                s, r, k = stage(MAXIMUM)
                                wait(pe, S["below"], s - 1)
                                maxima = bank(MAX[r % 2])[:, 0:TILES * 3 * HEADS]
                                pe.matmul(maxima, digit_w[:, :], zeros[:, :], start=True, stop=False, skip_group_check=True)
                                pick_pe(pe, S, picked, None, near, maxima.rearrange("p (j c) -> p j c", c=3 * HEADS), pick,
                                        lambda blk: [max_parts[:, bass.ds(blk, 1), :, :].rearrange("p a k c -> p (a k c)")])
                                pe.matmul(maxima, digit_w[:, :], zeros[:, :], start=False, stop=True,
                                          skip_group_check=True).then_inc(S["maxima"], 1)
                            if stage(SCATTER):
                                s, r, k = stage(SCATTER)
                                scatter_pe(pe, S, scattered, far, hot, vals[r], ACC_W, (S["vals"], s + 1))
                        slots(pe, SCATTER, body)

                    @block.scalar
                    def _(act):
                        picked = counter(act, "sm_picked", 1)
                        act.sem_inc(S["pick"], 1)

                        def body(stage):
                            ends = stage(0) and span("act", stage(0)[0])[0]
                            if stage(EXPONENT):
                                s, r, k = stage(EXPONENT)
                                act.wait_ge(S["below"], s + 1)
                                wait(act, S["vals_free"], s - (DEPTH - 1))
                                act.activation(vals[r][:, :, D:ACC_W], below[r % 2][:, :].rearrange("p (j h) -> p j h", h=HEADS),
                                               ACT.Exp).then_inc(S["weight"], 1)
                            if stage(0):
                                s, r, k = stage(0)
                                pick_act(act, S, picked, None, ends, dst[r][:, :], apart, pick, (S["dst_in"][r], 16 * (k + 1)))
                                act.sem_inc(S["picked"], 1)
                        slots(act, EXPONENT, body)

                    @block.vector
                    def _(dve):
                        scattered, before = counter(dve, "sm_scattered", 1), counter(dve, "sm_before", 0)
                        dve.sem_inc(S["pick_free"], 1)
                        number_nodes(None, dve, node_row, S["nodes"])
                        dve.memset(vals[0][:, :, :], 0.0)
                        dve.memset(hot[:, :, :], 0.0)
                        dve.memset(zeros[:, :], 0.0).then_inc(S["set"], 1)
                        dve.memset(acc[:, :, :], 0.0).then_inc(S["sums_free"], 1)
                        dve.wait_ge(S["sums_free"], 1)

                        def body(stage):
                            if stage(BELOW):
                                s, r, k = stage(BELOW)
                                dve.wait_ge(S["maxima"], s + 1)
                                wait(dve, S["weight"], s - 1)
                                maxima = bank(MAX[r % 2])[:, 0:TILES * 3 * HEADS].rearrange("p (j k h) -> p j k h", k=3, h=HEADS)
                                under = below[r % 2][:, :].rearrange("p (j h) -> p j h", h=HEADS)
                                whole = dve.tensor_reduce(top[r % 2][:, :], maxima.rearrange("p j k h -> p j h k"), AX.X, ALU.add)
                                whole.then_inc(S["maxima_used"], 1)
                                dve.wait_ge(S["maxima_used"], s + 1)
                                dve.tensor_tensor(under, logits[:, bass.ds(s, 1), :].rearrange("p a (j h) -> p (a j) h", h=HEADS),
                                                  top[r % 2][:, :].rearrange("p (j h) -> p j h", h=HEADS), ALU.subtract).then_inc(S["below"], 1)
                            if stage(WEIGHT):
                                s, r, k = stage(WEIGHT)
                                dve.wait_ge(S["weight"], s + 1)
                                dve.wait_ge(S["v_in"][r], 16 * (k + 1))
                                dve.tensor_tensor(vals[r][:, :, 0:D].rearrange("p j (h c) -> p j h c", c=HD),
                                                  v[r][:, :, :].rearrange("p j (h c) -> p j h c", c=HD),
                                                  vals[r][:, :, D:ACC_W].unsqueeze(3).to_broadcast([P, TILES, HEADS, HD]),
                                                  ALU.mult).then_inc(S["vals"], 1)
                            if stage(SCATTER):
                                s, r, k = stage(SCATTER)
                                scatter_dve(dve, S, scattered, before, span("dve", s)[0], s, node_row, hot, ACC_W)
                        slots(dve, SCATTER, body)
                        q = value(dve, scattered, 1)
                        dve.wait_ge(S["sums"], q)
                        add_sums(dve, S, q, before, ACC_W)

        project("tab1", [w_pair[0][:, 0, :], w_pair[0][:, 1, :]], [b1_row[0], None], src_table)
        end_phase()
        conv("conv1", 0)
        end_phase()
        time_vector(tvec)
        end_phase()
        node_update("node1", "L0_gnn_c1_w2", "L0_gnn_c1_b2", "L0_gnn_n1_g", "L0_gnn_n1_b", "time")
        end_phase()
        project("tab2", [w_pair[1][:, 0, :], w_pair[1][:, 1, :]], [b1_row[1], None], src_table)
        end_phase()
        conv("conv2", 1)
        end_phase()
        node_update("node2", "L0_gnn_c2_w2", "L0_gnn_c2_b2", "L0_gnn_n2_g", "L0_gnn_n2_b", "residual")
        end_phase()
        project("tab3", [w_qkv[:, r, :] for r in range(3)], [b_qkv[r] for r in range(3)], kv_table)
        end_phase()
        with nc.sbuf_tensor("logits", [P, SUPERS, TILES * HEADS], F32) as logits, \
                nc.sbuf_tensor("max_parts", [P, BLOCKS, 3, HEADS], BF16) as max_parts:
            with nc.sbuf_tensor("tops", [P, WINDOWS + 1], F32) as tops:
                logits_pass()
                end_phase()
                node_maxima()
                end_phase()
            softmax_pass()
            end_phase()
        node_update("node3", "L0_gnn_ow", "L0_gnn_ob", "L0_gnn_an_g", "L0_gnn_an_b", "out")
        end_phase()


_OUT = ((N_NODES, D), "float32")


def kernel(**inputs):
    import concourse.bacc as bacc
    from concourse.bass_utils import run_bass_kernel_spmd

    a = {k: np.asarray(v) for k, v in inputs.items()}
    x = np.zeros((NODES, D), a["x"].dtype)
    x[:N_NODES] = a.pop("x")
    src = np.zeros(EDGES, np.int32)
    src[:N_EDGES] = a.pop("src")
    dst = np.full(EDGES, N_NODES, np.int32)
    dst[:N_EDGES] = a.pop("dst")
    ea = np.zeros((EDGES, ED), a["edge_attr_4"].dtype)
    ea[:N_EDGES] = a.pop("edge_attr_4")
    arrays = {"x_rows": x,
              "src_idx": src.reshape(SUPERS, TILES, P).transpose(0, 2, 1),
              "dst_rows": dst.reshape(SUPERS, SUPER),
              "dst_cols": dst.reshape(SUPERS * TILES, P).T,
              "ea_rows": ea.T, **a}
    arrays = {f"in_{k}": np.ascontiguousarray(v) for k, v in arrays.items()}
    nc = bacc.Bacc("TRN2", target_bir_lowering=False, num_devices=1)
    io = {k[3:]: nc.dram_tensor(k, v.shape, mybir.dt.from_np(v.dtype), kind="ExternalInput").ap() for k, v in arrays.items()}
    out = nc.dram_tensor("out", _OUT[0], F32, kind="ExternalOutput").ap()
    build(nc, io, out)
    result = run_bass_kernel_spmd(nc, [arrays], core_ids=[0])
    return np.asarray(result.results[0]["out"])
```

```python
from contextlib import ExitStack

import numpy as np
import concourse.bass as bass
from concourse import mybir

F32 = mybir.dt.float32
BF16 = mybir.dt.bfloat16
I32 = mybir.dt.int32
ALU = mybir.AluOpType
ACT = mybir.ActivationFunctionType
AX = mybir.AxisListType

P = 128
N_NODES, N_EDGES, D = 6250, 200000, 128
HEADS, GROUPS, ED, TD = 8, 8, 4, 512
HD = D // HEADS
GC = D // GROUPS
BLOCKS = -(-N_NODES // P)
NODES = BLOCKS * P
TILES = 4
SUPER = TILES * P
DEPTH = 4
ITERS = -(-N_EDGES // (DEPTH * SUPER))
SUPERS = DEPTH * ITERS
EDGES = SUPERS * SUPER
CHUNK = 7
CHUNKS = BLOCKS // CHUNK
WIN = P // HEADS
WINDOWS = NODES // WIN
ACC_W = D + HEADS
TAB_P = SUPERS // 4
EPS = 1e-5
EA_SPLIT = P // ED
EA_COLS = EDGES // EA_SPLIT
CC = CHUNK * D
NEG = -1e30
RANGE_AT = (0, 6, 12, 21)
RANGE_BITS = (6, 6, 9, 9)
ROOT_SEED = 0x5f3759df
ROOT = (-5.148723380996802, 10.818224541572237, -12.019660736923178, 9.008935881668528)
ROOT_K = 0.2733154241963853
ROOT_STEPS = 8
PEN = 2.0 ** 50
assert CHUNKS * CHUNK == BLOCKS and TAB_P * 4 == SUPERS


def wait(eng, sem, value):
    if isinstance(value, int) and value <= 0:
        return
    eng.wait_ge(sem, value)


def hold(eng, sem, value, paced):
    if isinstance(value, int) and value <= 0:
        return
    eng.wait_ge(sem, value)
    eng.sem_inc(paced, 1)


def slots(eng, last_lag, body):
    def turn(i):
        for h in range(DEPTH):
            def stage(lag, h=h):
                back, r = divmod(h - lag, DEPTH)
                k = i + back
                if isinstance(k, int) and not 0 <= k < ITERS:
                    return None
                return DEPTH * k + r, r, k
            body(stage)

    tail = -(-last_lag // DEPTH)
    for i in range(tail + 1):
        turn(i)
    with eng.Fori(tail + 1, ITERS) as i:
        turn(i)
    for i in range(ITERS, ITERS + tail):
        turn(i)


def build(nc, io, out):
    ctx = ExitStack()
    with ctx:
        def sb(name, shape, dt=F32):
            return ctx.enter_context(nc.sbuf_tensor(name, shape, dt))

        live = []

        def sem(name):
            live.append(nc.alloc_semaphore(name))
            return live[-1]

        def end_phase():
            nc.clear_and_free_semaphores(live)
            live.clear()
            nc.all_engine_barrier()

        def dram(name, shape, dt=F32):
            return nc.dram_tensor(name, shape, dt, kind="Internal").ap()

        resid = dram("resid", [NODES, D])
        src_table = dram("src_table", [NODES, 3 * D], BF16)
        kv_table = dram("kv_table", [NODES, 2 * D])
        dst_rows = dram("dst_rows", [SUPERS, SUPER])
        dst_digits = dram("dst_digits", [2, EDGES], BF16)
        ea_parts = dram("ea_parts", [9 * ED, EDGES], BF16)
        w_parts_d = dram("w_parts_d", [2, 3 * ED, D], BF16)
        ranges_d = dram("ranges_d", [SUPERS], I32)
        v_edges = dram("v_edges", [SUPERS, P, TILES * D])
        max_nodes = dram("max_nodes", [NODES, HEADS])

        ps = ctx.enter_context(nc.psum_tensor("ps", [P, 8, 512], F32))

        def bank(k):
            return ps[:, k, :]

        def banks(k, cols):
            return ps[:, k:k + 2, :].rearrange("p a b -> p (a b)")[:, 0:cols]

        ident, ident_b = sb("ident", [P, P]), sb("ident_b", [P, P], BF16)
        iota_row = sb("iota_row", [P, P])
        node_of = sb("node_of", [P, BLOCKS])
        win_node = sb("win_node", [P, WINDOWS + 1])
        ranges = sb("ranges", [1, SUPERS], I32)
        dst_cols = sb("dst_cols", [P, SUPERS * TILES])
        digit_w = sb("digit_w", [2, P], BF16)
        neg_node = sb("neg_node", [P, BLOCKS])
        neg_win = sb("neg_win", [P, WINDOWS + 1])
        one_col = sb("one_col", [P, 1])
        dst_parts = sb("dst_parts", [P, BLOCKS, 3, D], BF16)
        acc = sb("acc", [P, BLOCKS, ACC_W])
        hidden = sb("hidden", [P, BLOCKS, D])
        w_pair = [sb(f"w_pair{n}", [P, 2, D]) for n in range(2)]
        w_edge = [sb(f"w_edge{n}", [9 * ED, D], BF16) for n in range(2)]
        b1_row = [sb(f"b1_row{n}", [P, D]) for n in range(2)]
        w_qkv, b_qkv = sb("w_qkv", [P, 3, D]), [sb(f"b_qkv{r}", [P, D]) for r in range(3)]
        tvec = sb("tvec", [P, D])

        def row_vector(name):
            return io[name].rearrange("(a n) -> a n", a=1).to_broadcast([P, D])

        def by_block(table, i):
            return table.rearrange("(b p) c -> p b c", p=P)[:, bass.ds(CHUNK * i, CHUNK), :]

        def row_of(row):
            return row[:, :].unsqueeze(1).to_broadcast([P, CHUNK, D])

        def chain(eng, step, base):
            count = [0]

            def done(ins):
                count[0] += 1
                ins.then_inc(step, 1)
                eng.wait_ge(step, base + count[0])
            return done

        def split_parts(dve, done, rest, to):
            for part in range(3):
                done(dve.tensor_copy(to[part], rest))
                if part < 2:
                    done(dve.tensor_tensor(rest, rest, to[part], ALU.subtract))

        def root_steps(dve, v, y, t, p):
            a, b_, c, d = ROOT
            return (lambda: dve.tensor_scalar(v, v, EPS, None, ALU.add),
                    lambda: dve.tensor_scalar(y.bitcast(I32), v.bitcast(I32), -0.5, float(ROOT_SEED), ALU.mult, ALU.add),
                    lambda: dve.tensor_tensor(t, y, y, ALU.mult),
                    lambda: dve.tensor_tensor(t, t, v, ALU.mult),
                    lambda: dve.scalar_tensor_tensor(p, t, a, t, ALU.add, ALU.mult),
                    lambda: dve.scalar_tensor_tensor(p, p, b_, t, ALU.add, ALU.mult),
                    lambda: dve.scalar_tensor_tensor(p, p, c, t, ALU.add, ALU.mult),
                    lambda: dve.scalar_tensor_tensor(y, p, d, y, ALU.add, ALU.mult))

        st = ExitStack()
        pid_i = st.enter_context(nc.sbuf_tensor("pid_i", [P, 1], I32))
        pid_f = st.enter_context(nc.sbuf_tensor("pid_f", [P, 1], F32))
        iota_i = st.enter_context(nc.sbuf_tensor("iota_i", [P, P], I32))
        node_i = st.enter_context(nc.sbuf_tensor("node_i", [P, BLOCKS], I32))
        win_i = st.enter_context(nc.sbuf_tensor("win_i", [P, WINDOWS + 1], I32))
        lane_i = st.enter_context(nc.sbuf_tensor("lane_i", [P, 1], I32))
        lane_f = st.enter_context(nc.sbuf_tensor("lane_f", [P, 1], F32))
        rows_i = st.enter_context(nc.sbuf_tensor("rows_i", [TAB_P, 4 * SUPER], I32))
        digit_i = st.enter_context(nc.sbuf_tensor("digit_i", [TAB_P, 2, 4 * SUPER], I32))
        digit_b = st.enter_context(nc.sbuf_tensor("digit_b", [TAB_P, 2, 4 * SUPER], BF16))
        rows_f = st.enter_context(nc.sbuf_tensor("rows_f", [TAB_P, 4, SUPER], F32))
        ends_f = st.enter_context(nc.sbuf_tensor("ends_f", [TAB_P, 4, 2], F32))
        ends_i = st.enter_context(nc.sbuf_tensor("ends_i", [TAB_P, 4, 2], I32))
        range_i = st.enter_context(nc.sbuf_tensor("range_i", [TAB_P, 4, 4], I32))
        range_f = st.enter_context(nc.sbuf_tensor("range_f", [TAB_P, 4, 4], F32))
        range_o = st.enter_context(nc.sbuf_tensor("range_o", [TAB_P, 4, 4], I32))
        word = st.enter_context(nc.sbuf_tensor("word", [TAB_P, 4], I32))
        cols_i = st.enter_context(nc.sbuf_tensor("cols_i", [P, SUPERS * TILES], I32))
        w_raw = st.enter_context(nc.sbuf_tensor("w_raw", [P, 8, D], F32))
        w_mean = st.enter_context(nc.sbuf_tensor("w_mean", [P, 8, GROUPS], F32))
        w_edge_f = st.enter_context(nc.sbuf_tensor("w_edge_f", [ED, 2, D], F32))
        w_edge_b = st.enter_context(nc.sbuf_tensor("w_edge_b", [ED, 2, 3, D], BF16))
        ea_f = acc[:, :, :].rearrange("p b c -> p (b c)")[:, 0:EA_COLS]
        ea_b = dst_parts[:, :, :, :].rearrange("p b k c -> p (b k c)").rearrange("p (a e) -> p a e", a=3)
        with st:
            iota_done, dst_in, weights_in, step = sem("iota_done"), sem("dst_in"), sem("weights_in"), sem("setup_step")
            digits_out, ranges_out, ranges_in = sem("digits_out"), sem("ranges_out"), sem("ranges_in")
            rows_out, ea_in, ea_cut, ea_left, ea_out = (sem(x) for x in ("rows_out", "ea_in", "ea_cut", "ea_left", "ea_out"))
            w_split, w_out, w_edge_in, x_in = (sem(x) for x in ("w_split", "w_out", "w_edge_in", "x_in"))
            with nc.Block() as block:
                @block.gpsimd
                def _(pool):
                    pool.iota(pid_i[:, :], [[0, 1]], base=0, channel_multiplier=1).then_inc(iota_done, 1)
                    pool.iota(iota_i[:, :], [[1, P]], base=0, channel_multiplier=0).then_inc(iota_done, 1)
                    pool.iota(node_i[:, :], [[P, BLOCKS]], base=0, channel_multiplier=1).then_inc(iota_done, 1)
                    pool.iota(win_i[:, :], [[WIN, WINDOWS + 1]], base=0, channel_multiplier=0).then_inc(iota_done, 1)

                @block.sync
                def _(sp):
                    sp.dma_start(rows_i[:, :], io["dst_rows"].rearrange("(p c) e -> p (c e)", c=4)).then_inc(dst_in, 16)
                    sp.dma_start(cols_i[:, :], io["dst_cols"]).then_inc(dst_in, 16)
                    sp.dma_start(hidden[:, :, :], io["x_rows"].rearrange("(b p) c -> p b c", p=P)).then_inc(x_in, 16)
                    sp.dma_start(ea_f, io["ea_rows"].rearrange("c (q e) -> (c q) e", q=EA_SPLIT)).then_inc(ea_in, 16)
                    for n in range(2):
                        w1 = io[f"L0_gnn_c{n + 1}_w1"]
                        for half in range(2):
                            sp.dma_start(w_raw[:, 4 * n + half, :], w1[half * D:(half + 1) * D, :]).then_inc(weights_in, 16)
                        sp.dma_start(w_raw[0:ED, 4 * n + 2, :], w1[2 * D:2 * D + ED, :]).then_inc(weights_in, 16)
                        sp.dma_start(w_raw[:, 4 * n + 3, :], row_vector(f"L0_gnn_c{n + 1}_b1")).then_inc(weights_in, 16)
                    for r, x in enumerate("qkv"):
                        sp.dma_start(w_qkv[:, r, :], io[f"L0_gnn_{x}w"]).then_inc(weights_in, 16)
                        sp.dma_start(b_qkv[r][:, :], row_vector(f"L0_gnn_{x}b")).then_inc(weights_in, 16)
                    sp.wait_ge(step, 1)
                    sp.dma_start(dst_rows.rearrange("(p c) e -> p (c e)", c=4), rows_f[:, :, :].rearrange("p c e -> p (c e)")).then_inc(rows_out, 16)
                    sp.wait_ge(step, 5)
                    for d in range(2):
                        sp.dma_start(dst_digits[d, :].rearrange("(p e) -> p e", p=TAB_P), digit_b[:, d, :]).then_inc(digits_out, 16)
                    sp.wait_ge(step, 20)
                    sp.dma_start(ranges_d.rearrange("(p c) -> p c", c=4), word[:, :]).then_inc(ranges_out, 16)
                    sp.wait_ge(ranges_out, 16)
                    sp.dma_start(ranges[:, :], ranges_d.rearrange("(a s) -> a s", a=1)).then_inc(ranges_in, 16)
                    sp.wait_ge(w_split, 10)
                    for n in range(2):
                        sp.dma_start(w_parts_d[n, :, :].rearrange("(p c) d -> c p d", c=ED), w_edge_b[:, n, :, :]).then_inc(w_out, 16)
                    sp.wait_ge(w_out, 32)
                    for n in range(2):
                        for part in range(3):
                            sp.dma_start(w_edge[n][3 * ED * part:3 * ED * (part + 1), :], w_parts_d[n, :, :]).then_inc(w_edge_in, 16)
                    sp.wait_ge(ea_cut, 3)
                    for part in range(3):
                        for w_part in range(3):
                            row = ED * (3 * part + w_part)
                            sp.dma_start(ea_parts[row:row + ED, :].rearrange("c (q e) -> (c q) e", q=EA_SPLIT), ea_b[:, part, :]).then_inc(ea_out, 16)
                    sp.wait_ge(rows_out, 16)
                    sp.wait_ge(digits_out, 32)
                    sp.wait_ge(ranges_in, 16)
                    sp.wait_ge(w_edge_in, 96)

                @block.scalar
                def _(act):
                    act.wait_ge(ea_in, 16)
                    act.activation(ea_b[:, 0, :], ea_f, ACT.Copy).then_inc(ea_cut, 1)
                    for part in range(1, 3):
                        act.wait_ge(ea_left, part)
                        act.activation(ea_b[:, part, :], ea_f, ACT.Copy).then_inc(ea_cut, 1)

                @block.vector
                def _(dve):
                    count = [0]

                    def done(ins):
                        count[0] += 1
                        ins.then_inc(step, 1)
                        dve.wait_ge(step, count[0])

                    dve.wait_ge(dst_in, 32)
                    done(dve.tensor_copy(rows_f[:, :, :].rearrange("p c e -> p (c e)"), rows_i[:, :]))
                    done(dve.tensor_scalar(digit_i[:, 0, :], rows_i[:, :], 7, None, ALU.arith_shift_right))
                    done(dve.tensor_scalar(digit_i[:, 1, :], rows_i[:, :], P - 1, None, ALU.bitwise_and))
                    done(dve.tensor_copy(digit_b[:, 0, :], digit_i[:, 0, :]))
                    done(dve.tensor_copy(digit_b[:, 1, :], digit_i[:, 1, :]))
                    done(dve.tensor_reduce(ends_f[:, :, 0], rows_f[:, :, :], AX.X, ALU.min))
                    done(dve.tensor_reduce(ends_f[:, :, 1], rows_f[:, :, :], AX.X, ALU.max))
                    done(dve.tensor_copy(ends_i[:, :, :], ends_f[:, :, :]))
                    done(dve.tensor_scalar(range_i[:, :, 0:2], ends_i[:, :, :], 7, None, ALU.arith_shift_right))
                    done(dve.tensor_scalar(range_i[:, :, 2:4], ends_i[:, :, :], 4, None, ALU.arith_shift_right))
                    done(dve.tensor_copy(range_f[:, :, :], range_i[:, :, :]))
                    ends = range_f[:, :, :].rearrange("p c (t e) -> p (c t) e", e=2)[:, :, 1]
                    done(dve.tensor_scalar(ends, ends, 1.0, None, ALU.add))
                    done(dve.tensor_copy(range_o[:, :, :], range_f[:, :, :]))
                    for n in range(1, 4):
                        done(dve.tensor_scalar(range_o[:, :, n], range_o[:, :, n], RANGE_AT[n], None, ALU.logical_shift_left))
                        done(dve.tensor_tensor(range_o[:, :, 0], range_o[:, :, 0], range_o[:, :, n], ALU.bitwise_or))
                    done(dve.tensor_copy(word[:, :], range_o[:, :, 0]))
                    done(dve.tensor_copy(dst_cols[:, :], cols_i[:, :]))
                    dve.wait_ge(iota_done, 4)
                    done(dve.tensor_copy(pid_f[:, :], pid_i[:, :]))
                    done(dve.tensor_copy(iota_row[:, :], iota_i[:, :]))
                    done(dve.tensor_scalar(ident[:, :], iota_row[:, :], pid_f[:, 0:1], None, ALU.is_equal))
                    done(dve.tensor_copy(ident_b[:, :], ident[:, :]))
                    for part in range(1, 3):
                        dve.wait_ge(ea_cut, part)
                        dve.tensor_tensor(ea_f, ea_f, ea_b[:, part - 1, :], ALU.subtract).then_inc(ea_left, 1)
                    done(dve.tensor_copy(node_of[:, :], node_i[:, :]))
                    done(dve.tensor_copy(win_node[:, :], win_i[:, :]))
                    done(dve.tensor_scalar(lane_i[:, :], pid_i[:, :], WIN - 1, None, ALU.bitwise_and))
                    done(dve.tensor_copy(lane_f[:, :], lane_i[:, :]))
                    done(dve.tensor_scalar(win_node[:, :], win_node[:, :], lane_f[:, 0:1], None, ALU.add))
                    done(dve.tensor_scalar(digit_w[:, :], iota_row[0:2, :], 0.0, 1.0, ALU.mult, ALU.add))
                    done(dve.memset(digit_w[0:1, :], float(P)))
                    done(dve.tensor_scalar(neg_node[:, :], node_of[:, :], -1.0, None, ALU.mult))
                    done(dve.tensor_scalar(neg_win[:, :], win_node[:, :], -PEN, None, ALU.mult))
                    done(dve.memset(one_col[:, :], 1.0))
                    dve.wait_ge(weights_in, 224)
                    for n in range(2):
                        for r, rows in ((0, P), (1, P), (2, ED), (3, P)):
                            w = w_raw[0:rows, 4 * n + r, :].rearrange("p (g c) -> p g c", c=GC)
                            mean = w_mean[0:rows, 4 * n + r, :]
                            to = (w_pair[n][:, 0, :], w_pair[n][:, 1, :], w_edge_f[:, n, :], b1_row[n][:, :])[r]
                            done(dve.tensor_reduce(mean, w, AX.X, ALU.add))
                            done(dve.tensor_scalar(mean, mean, -1.0 / GC, None, ALU.mult))
                            done(dve.tensor_tensor(to.rearrange("p (g c) -> p g c", c=GC), w,
                                                   mean.unsqueeze(2).to_broadcast([rows, GROUPS, GC]), ALU.add))
                    split = chain(dve, w_split, 0)
                    for n in range(2):
                        split_parts(dve, split, w_edge_f[:, n, :], [w_edge_b[:, n, part, :] for part in range(3)])

        with ExitStack() as st:
            def b(name, shape, dt=F32):
                return st.enter_context(nc.sbuf_tensor(f"ln_{name}", shape, dt))

            sq, mean = b("sq", [P, CHUNK, D]), b("mean", [P, CHUNK])
            var, rstd, root_t, root_p = (b(x, [P, BLOCKS]) for x in ("var", "rstd", "root_t", "root_p"))
            step, centred, squared, ready, kept, paced = (sem(f"ln_{n}") for n in ("step", "centred", "squared", "ready", "kept", "paced"))
            STEPS = 4
            with nc.Block() as block:
                @block.vector
                def _(dve):
                    dve.wait_ge(x_in, 16)
                    wide = lambda v: v.unsqueeze(2).to_broadcast([P, CHUNK, D])
                    with dve.Fori(0, CHUNKS) as i:
                        done = chain(dve, step, STEPS * i)
                        blocks = bass.ds(CHUNK * i, CHUNK)
                        x = hidden[:, blocks, :]
                        done(dve.tensor_reduce(mean[:, :], x, AX.X, ALU.add))
                        done(dve.tensor_scalar(mean[:, :], mean[:, :], -1.0 / D, None, ALU.mult))
                        done(dve.tensor_tensor(x, x, wide(mean[:, :]), ALU.add))
                        dve.sem_inc(centred, 1)
                        dve.wait_ge(squared, i + 1)
                        done(dve.tensor_reduce(var[:, blocks], sq[:, :, :], AX.X, ALU.add))
                    done = chain(dve, step, STEPS * CHUNKS)
                    for root_step in root_steps(dve, var[:, :], rstd[:, :], root_t[:, :], root_p[:, :]):
                        done(root_step())
                    done(dve.tensor_scalar(rstd[:, :], rstd[:, :], ROOT_K, None, ALU.mult))
                    with dve.Fori(0, CHUNKS) as i:
                        blocks = bass.ds(CHUNK * i, CHUNK)
                        dve.scalar_tensor_tensor(hidden[:, blocks, :], hidden[:, blocks, :], 0.0, wide(rstd[:, blocks]),
                                                 ALU.max, ALU.mult).then_inc(ready, 1)

                @block.scalar
                def _(act):
                    with act.Fori(0, CHUNKS) as i:
                        hold(act, centred, i + 1, paced)
                        act.activation(sq[:, :, :], hidden[:, bass.ds(CHUNK * i, CHUNK), :], ACT.Square, scale=D ** -0.5).then_inc(squared, 1)

                @block.sync
                def _(sp):
                    sp.wait_ge(ready, CHUNKS)
                    sp.dma_start(resid.rearrange("(b p) c -> p b c", p=P), hidden[:, :, :]).then_inc(kept, 16)
                    sp.wait_ge(ea_out, 144)

        def project(tag, weights, biases, table, stores=()):
            n = len(weights)
            in_parts = n == 2
            with ExitStack() as st:
                def b(name, shape, dt=F32):
                    return st.enter_context(nc.sbuf_tensor(f"{tag}_{name}", shape, dt))

                stage, hT = b("stage", [P, CHUNK, D]), b("hT", [P, CC])
                rest = [b(f"rest{r}", [P, CHUNK, D]) for r in range(2 if in_parts else 1)]
                outs = b("outs", [P, CHUNK, 3 * D], BF16) if in_parts else b("outs", [P, CHUNK, (n - 1) * D])
                staged, hT_ps, hT_done, stored, left, cut, paced = (
                    sem(f"{tag}_{x}") for x in ("staged", "hT_ps", "hT", "stored", "left", "cut", "paced"))
                part_ps = [sem(f"{tag}_part_ps{r}") for r in range(n)]
                part_free = [sem(f"{tag}_part_free{r}") for r in range(n)]
                trans = banks(0, CC)
                parts = [banks(2 + 2 * r, CC).rearrange("p (k c) -> p k c", c=D) for r in range(n)]
                products = len(rest)
                STEPS = 3 * products

                def cut_of(i):
                    to = [[dst_parts[:, bass.ds(CHUNK * i, CHUNK), p, :] for p in range(3)]]
                    return to + [[outs[:, :, p * D:(p + 1) * D] for p in range(3)]] if in_parts else to

                with nc.Block() as block:
                    @block.scalar
                    def _(act):
                        def set_stage(i):
                            act.activation(stage[:, :, :], hidden[:, bass.ds(CHUNK * i, CHUNK), :], ACT.Copy).then_inc(staged, 1)

                        def flip(i, more):
                            act.wait_ge(hT_ps, i + 1)
                            act.activation(hT[:, :], trans, ACT.Copy).then_inc(hT_done, 1)
                            if more:
                                set_stage(i + 1)

                        def chunk(i, coming):
                            for p in range(3):
                                for r in range(products):
                                    hold(act, left, STEPS * i + products * p + r + 1, paced)
                                    if r == 1 and p == 0:
                                        act.wait_ge(stored, 16 * i + 16)
                                    act.activation(cut_of(i)[r][p], rest[r][:, :, :], ACT.Copy).then_inc(cut, 1)
                                if p == 0 and coming:
                                    hold(act, part_ps[n - 1], i + 1, paced)
                                    flip(i + 1, coming > 1)

                        set_stage(0)
                        flip(0, True)
                        with act.Fori(0, CHUNKS - 2) as i:
                            chunk(i, 2)
                        chunk(CHUNKS - 2, 1)
                        chunk(CHUNKS - 1, 0)

                    @block.tensor
                    def _(pe):
                        with pe.Fori(0, CHUNKS) as i:
                            pe.wait_ge(staged, i + 1)
                            for k in range(CHUNK):
                                last = pe.transpose(trans[:, k * D:(k + 1) * D], stage[:, k, :], ident[:, :])
                            last.then_inc(hT_ps, 1)
                            pe.wait_ge(hT_done, i + 1)
                            for r in range(n):
                                pe.wait_ge(part_free[r], i + 1)
                                for k in range(CHUNK):
                                    last = pe.matmul(parts[r][:, k, :], hT[:, k * D:(k + 1) * D], weights[r],
                                                     start=True, stop=True)
                                last.then_inc(part_ps[r], 1)

                    @block.vector
                    def _(dve):
                        for r in range(n):
                            dve.sem_inc(part_free[r], 1)
                        with dve.Fori(0, CHUNKS) as i:
                            to = cut_of(i)
                            for r in range(products):
                                dve.wait_ge(part_ps[r], i + 1)
                                if biases[r] is None:
                                    dve.tensor_copy(rest[r][:, :, :], parts[r]).then_inc(left, 1)
                                else:
                                    dve.tensor_tensor(rest[r][:, :, :], parts[r], row_of(biases[r]), ALU.add).then_inc(left, 1)
                                dve.wait_ge(left, STEPS * i + r + 1)
                                dve.sem_inc(part_free[r], 1)
                            if not in_parts:
                                dve.wait_ge(stored, 16 * i + 16)
                                for r in range(1, n):
                                    dve.wait_ge(part_ps[r], i + 1)
                                    dve.tensor_tensor(outs[:, :, (r - 1) * D:r * D], parts[r], row_of(biases[r]),
                                                      ALU.add).then_inc(part_free[r], 1)
                            for p in range(2):
                                for r in range(products):
                                    dve.wait_ge(cut, STEPS * i + products * p + r + 1)
                                    dve.tensor_tensor(rest[r][:, :, :], rest[r][:, :, :], to[r][p], ALU.subtract).then_inc(left, 1)
                            dve.wait_ge(cut, STEPS * (i + 1))

                    @block.sync
                    def _(sp):
                        sp.sem_inc(stored, 16)
                        with sp.Fori(0, CHUNKS) as i:
                            hold(sp, cut, STEPS * (i + 1), paced)
                            if not in_parts:
                                hold(sp, part_free[n - 1], i + 2, paced)
                            sp.dma_start(by_block(table, i), outs[:, :, :]).then_inc(stored, 16)
                        sp.wait_ge(stored, 16 * (CHUNKS + 1))
                        for count, full in stores:
                            sp.wait_ge(count, full)

        ENGINES = {"pe": mybir.EngineType.PE, "act": mybir.EngineType.Activation, "dve": mybir.EngineType.DVE}

        def span(eng, s):
            word = nc.values_load(ranges[0:1, bass.ds(s, 1)], engines=(ENGINES[eng],), min_val=0, max_val=2 ** 30 - 1,
                                  skip_runtime_bounds_check_because="made on the chip of dst, which lies in the nodes")
            part = lambda n, low, high: ((word >> RANGE_AT[n]) & (2 ** RANGE_BITS[n] - 1)).with_bounds(min_val=low, max_val=high)
            return ((part(0, 0, BLOCKS - 1), part(1, 1, BLOCKS)), (part(2, 0, WINDOWS - 1), part(3, 1, WINDOWS)))

        def span_registers(eng, tag):
            return [[eng.alloc_register(f"{tag}_{end}{r}") for end in ("first", "end")] for r in range(DEPTH)]

        def keep_span(eng, kept, ends):
            for reg, end in zip(kept, ends):
                eng.reg_mov(reg, end)
            return kept_span(eng, kept)

        def kept_span(eng, kept):
            return value(eng, kept[0], 0, BLOCKS - 1), value(eng, kept[1], 1, BLOCKS)

        def pairs(eng, ends, body, step=1):
            with eng.Fori(*ends, step) as n:
                body(n)

        def counter(eng, name, start):
            reg = eng.alloc_register(name)
            eng.reg_mov(reg, start)
            return reg

        def value(eng, reg, low, high=BLOCKS * SUPERS + 8):
            return eng.snap(reg, min_val=low, max_val=high)

        def edge_sems(tag, names, loads):
            t = {x: sem(f"{tag}_{x}") for x in names}
            t.update({x: [sem(f"{tag}_{x}{r}") for r in range(DEPTH)] for x in loads})
            return t

        class Picks:

            def __init__(self, tag, buffers):
                self.tag, self.buffers = tag, buffers
                self.made, self.used, self.apart_made = (sem(f"{tag}_{x}") for x in ("pick", "pick_free", "apart"))

            def counters(self, eng):
                return counter(eng, f"{self.tag}_picked", 1), counter(eng, f"{self.tag}_turn", 0)

            def buffer(self, eng, turn):
                return self.buffers[:, bass.ds(value(eng, turn, 0, 1), 1), :].rearrange("p a e -> p (a e)")

        def next_pair(eng, reg, turn):
            eng.reg_sub(turn, 1, turn)
            eng.reg_add(reg, reg, 1)

        def pick_act(act, S, picks, counters, ends, dst, apart, ready):
            reg, turn = counters

            def body(blk):
                q = value(act, reg, 1)
                act.wait_ge(*ready)
                hold(act, picks.made, q, S["act_paced"])
                act.activation(apart, dst, ACT.Square, bias=neg_node[:, bass.ds(blk, 1)]).then_inc(picks.apart_made, 1)
                act.wait_ge(picks.used, q)
                hold(act, picks.apart_made, q, S["act_paced"])
                act.activation(picks.buffer(act, turn), apart, ACT.Relu, bias=one_col[:, 0:1], scale=-1.0).then_inc(picks.made, 1)
                next_pair(act, reg, turn)
            pairs(act, ends, body)

        def pick_pe(pe, picks, counters, ends, to, rows):
            reg, turn = counters

            def body(blk):
                q = value(pe, reg, 1)
                half, table = bass.ds(value(pe, turn, 0, 1), 1), rows(blk)
                pe.wait_ge(picks.made, q + 1)
                for j in range(TILES):
                    for part in table:
                        names = picks.buffers[:, half, j * P:(j + 1) * P].rearrange("p a e -> p (a e)")
                        last = pe.matmul(to[:, j, :], names, part, start=False, stop=False, skip_group_check=True)
                last.then_inc(picks.used, 1)
                next_pair(pe, reg, turn)
            pairs(pe, ends, body)

        def parts_of_dst(blk):
            return [dst_parts[:, bass.ds(blk, 1), part, :].rearrange("p a c -> p (a c)") for part in range(3)]

        class Scatter:

            def __init__(self, tag, S, hot, width, spare):
                self.tag, self.S, self.hot, self.width, self.spare = tag, S, hot, width, spare

            def counters(self, eng):
                names = ("scattered", "fresh", "start") if len(self.hot) == 2 else ("scattered",)
                return [counter(eng, f"{self.tag}_{name}", 1) for name in names]

            def enter(self, eng, counters):
                if len(counters) > 1:
                    reg, fresh, start = counters
                    eng.reg_mov(fresh, start)
                    eng.reg_mov(start, reg)

            def step(self, eng, counters):
                eng.reg_add(counters[0], counters[0], 1)
                if len(counters) > 1:
                    eng.reg_mov(counters[1], counters[0])

            def names(self, dve, counters, before, ends, s, r, node_row):
                S, hot = self.S, self.hot[r % len(self.hot)]
                self.enter(dve, counters)

                def body(blk):
                    q = value(dve, counters[0], 1)
                    dve.wait_ge(S["sums"], value(dve, counters[1], 1) if len(counters) > 1 else q)
                    dve.tensor_tensor(hot[:, :, :], node_row[:, bass.ds(blk, 1), :].to_broadcast([P, TILES, P]),
                                      dst_cols[:, bass.ds(TILES * s, TILES)].unsqueeze(2).to_broadcast([P, TILES, P]),
                                      ALU.is_equal).then_inc(S["hot"], 1)
                    self.add(dve, q, before)
                    dve.reg_mov(before[0], blk)
                    if len(counters) > 1:
                        dve.reg_mov(before[1], r % 2)
                    self.step(dve, counters)
                pairs(dve, ends, body)

            def add(self, dve, q, before):
                S = self.S
                if len(self.hot) == 2:
                    dve.wait_ge(S["sums"], q)
                dve.wait_ge(S["sums_free"], q)
                to = acc[:, bass.ds(value(dve, before[0], 0, BLOCKS - 1), 1), 0:self.width].rearrange("p a c -> p (a c)")
                sums = bank(SUMS[0])[:, 0:self.width]
                if len(self.hot) == 2:
                    sums = ps[:, bass.ds(value(dve, before[1], 0, 1) + SUMS[0], 1), 0:self.width].rearrange("p a c -> p (a c)")
                dve.tensor_tensor(to, sums, to, ALU.add).then_inc(S["sums_free"], 1)

            def products(self, pe, counters, ends, r, vals, ready):
                S, g = self.S, r % len(self.hot)
                self.enter(pe, counters)

                def body(blk):
                    q = value(pe, counters[0], 1)
                    pe.wait_ge(*ready)
                    pe.wait_ge(S["hot"], q)
                    pe.wait_ge(S["sums_free"], (value(pe, counters[1], 1) if len(counters) > 1 else q) + 1)
                    for j in range(TILES):
                        last = pe.matmul(bank(SUMS[g])[:, 0:self.width], self.hot[g][:, j, :], vals[:, j, 0:self.width],
                                         start=(j == 0), stop=(j == TILES - 1))
                    last.then_inc(S["sums"], 1)
                    self.step(pe, counters)
                pairs(pe, ends, body)
                pe.matmul(bank(self.spare)[:, 0:1], ident[:, :], ident[:, 0:1], start=True, stop=True).then_inc(S["vals_free"], 1)

        SUMS = (6, 7)

        def number_nodes(pool, dve, node_row, made):
            if pool:
                pool.iota(node_row[:, :, :].bitcast(I32), [[P, BLOCKS], [1, P]], base=0, channel_multiplier=0).then_inc(made, 1)
            if dve:
                dve.wait_ge(made, 1)
                dve.tensor_copy(node_row[:, :, :], node_row[:, :, :].bitcast(I32)).then_inc(made, 1)
                dve.wait_ge(made, 2)

        def conv(tag, layer):
            with ExitStack() as st:
                def b(name, shape, dt=F32):
                    return st.enter_context(nc.sbuf_tensor(f"{tag}_{name}", shape, dt))

                def b2(name, shape, dt=F32):
                    return [b(f"{name}{g}", shape, dt) for g in range(2)]

                def deep(name, shape, dt=F32):
                    return [b(f"{name}{r}", shape, dt) for r in range(DEPTH)]

                idx, dst, ea = deep("idx", [P, TILES], I32), deep("dst", [P, SUPER]), deep("ea", [9 * ED, SUPER], BF16)
                rows = deep("rows", [P, TILES, 3 * D], BF16)
                apart, picks = b("apart", [P, SUPER]), Picks(tag, b("pick", [P, 2, SUPER], BF16))
                sq = b2("sq", [P, TILES * D])
                var, root_t, root_p = (b(x, [P, 2, TILES * GROUPS]) for x in ("var", "root_t", "root_p"))
                rstd = b2("rstd", [P, 2, TILES * GROUPS])
                y, vals = b2("y", [P, TILES, D]), b2("vals", [P, TILES, D + 1])
                hot, node_row = [b("hot", [P, TILES, P])], b("node_row", [P, BLOCKS, P])
                gamma, beta = b("gamma", [P, D]), b("beta", [P, D])
                beta_parts, beta_rows, ones_b = b("beta_parts", [P, 3, D], BF16), b("beta_rows", [P, D], BF16), b("ones_b", [P, P], BF16)
                S = edge_sems(tag, ("affine_in", "nodes", "hot", "sums", "sums_free", "ones",
                                    "sp_paced", "pool_paced", "act_paced", "beta_step", "picked", "rows_free", "message",
                                    "sq", "ssq", "root", "scaled", "gained", "y", "vals", "vals_free"),
                              ("idx_in", "dst_in", "ea_in", "rows_in"))
                scatter = Scatter(tag, S, hot, D + 1, 7)
                MSG, SHIFT = (0, 1, 2, 3), (4, 5)
                MESSAGE, SQUARE, VARIANCE, SCALE, ADD_BETA, SILU, SCATTER = 1, 2, 2, 4, 4, 5, 5
                grouped = [TILES * GROUPS, GC]
                BETA_STEPS = 9
                with nc.Block() as block:
                    @block.sync
                    def _(sp):
                        sp.dma_start(gamma[:, :], row_vector(f"L0_gnn_c{layer + 1}_g")).then_inc(S["affine_in"], 16)
                        sp.dma_start(beta[:, :], row_vector(f"L0_gnn_c{layer + 1}_bt")).then_inc(S["affine_in"], 16)

                        def body(stage):
                            s, r, k = stage(0)
                            hold(sp, S["rows_in"][r], 16 * TILES * k, S["sp_paced"])
                            sp.dma_start(idx[r][:, :], io["src_idx"][bass.ds(s, 1), :, :].rearrange("a p j -> (a p) j")).then_inc(S["idx_in"][r], 16)
                            hold(sp, S["picked"], s - (DEPTH - 1), S["sp_paced"])
                            sp.dma_start(dst[r][:, :], dst_rows[bass.ds(s, 1), :].to_broadcast([P, SUPER])).then_inc(S["dst_in"][r], 16)
                            hold(sp, S["message"], s - (DEPTH - 1), S["sp_paced"])
                            sp.dma_start(ea[r][:, :], ea_parts[:, bass.ds(s * SUPER, SUPER)]).then_inc(S["ea_in"][r], 16)
                        slots(sp, 0, body)

                    @block.gpsimd
                    def _(pool):
                        number_nodes(pool, None, node_row, S["nodes"])

                        def body(stage):
                            s, r, k = stage(0)
                            hold(pool, S["idx_in"][r], 16 * (k + 1), S["pool_paced"])
                            hold(pool, S["rows_free"], s - (DEPTH - 1), S["pool_paced"])
                            for j in range(TILES):
                                pool.indirect_dma_start(
                                    rows[r][:, j, :], None, src_table,
                                    bass.IndirectOffsetOnAxis(idx[r][:, j:j + 1], 0)).then_inc(S["rows_in"][r], 16)
                        slots(pool, 0, body)

                    @block.tensor
                    def _(pe):
                        picked, scattered = picks.counters(pe), scatter.counters(pe)
                        kept = span_registers(pe, tag)
                        pe.wait_ge(S["beta_step"], BETA_STEPS)
                        pe.wait_ge(S["ones"], 1)
                        pe.matmul(bank(SUMS[0])[:, 0:D + 1], hot[0][:, 0, :], vals[0][:, 0, :], start=True, stop=True).then_inc(S["sums"], 1)

                        def body(stage):
                            far = stage(SCATTER) and kept_span(pe, kept[stage(SCATTER)[1]])
                            near = stage(MESSAGE) and keep_span(pe, kept[stage(MESSAGE)[1]], span("pe", stage(MESSAGE)[0])[0])
                            if stage(MESSAGE):
                                s, r, k = stage(MESSAGE)
                                pe.wait_ge(S["rows_in"][r], 16 * TILES * (k + 1))
                                wait(pe, S["scaled"], s - (DEPTH - 1))
                                for p in range(3):
                                    last = pe.matmul(bank(MSG[r]).rearrange("p (j c) -> p j c", c=D), ident_b[:, :], rows[r][:, :, p * D:(p + 1) * D],
                                                     start=(p == 0), stop=False, skip_group_check=True)
                                last.then_inc(S["rows_free"], 1)
                                pe.wait_ge(S["ea_in"][r], 16 * (k + 1))

                                def edge_part(j):
                                    return pe.matmul(bank(MSG[r])[:, j * D:(j + 1) * D], ea[r][:, j * P:(j + 1) * P],
                                                     w_edge[layer][:, :], start=False, stop=(j == TILES - 1), skip_group_check=True)

                                for j in range(TILES - 1):
                                    edge_part(j)
                                pick_pe(pe, picks, picked, near, bank(MSG[r]).rearrange("p (j c) -> p j c", c=D), parts_of_dst)
                                edge_part(TILES - 1).then_inc(S["message"], 1)
                            if stage(ADD_BETA):
                                s, r, k = stage(ADD_BETA)
                                wait(pe, S["vals"], s - 1)
                                pe.matmul(bank(SHIFT[r % 2]).rearrange("p (j c) -> p j c", c=D), ones_b[:, :],
                                          beta_rows[:, :].unsqueeze(1).to_broadcast([P, TILES, D]), start=True, stop=False, skip_group_check=True)
                                pe.wait_ge(S["gained"], s + 1)
                                pe.matmul(bank(SHIFT[r % 2]).rearrange("p (j c) -> p j c", c=D), ident[:, :], y[r % 2][:, :, :],
                                          start=False, stop=True, skip_group_check=True).then_inc(S["y"], 1)
                            if stage(SCATTER):
                                s, r, k = stage(SCATTER)
                                scatter.products(pe, scattered, far, r, vals[r % 2], (S["vals"], s + 1))
                        slots(pe, SCATTER, body)

                    @block.scalar
                    def _(act):
                        picked = picks.counters(act)
                        act.sem_inc(picks.made, 1)

                        def body(stage):
                            ends = stage(0) and span("act", stage(0)[0])[0]
                            if stage(SQUARE):
                                s, r, k = stage(SQUARE)
                                act.wait_ge(S["message"], s + 1)
                                wait(act, S["ssq"], s - 1)
                                act.activation(sq[r % 2][:, :], bank(MSG[r]), ACT.Square, scale=GC ** -0.5).then_inc(S["sq"], 1)
                            if stage(SILU):
                                s, r, k = stage(SILU)
                                act.wait_ge(S["y"], s + 1)
                                wait(act, S["vals_free"], s - 1)
                                act.activation(vals[r % 2][:, :, 0:D], bank(SHIFT[r % 2]).rearrange("p (j c) -> p j c", c=D), ACT.Silu).then_inc(S["vals"], 1)
                            if stage(0):
                                s, r, k = stage(0)
                                pick_act(act, S, picks, picked, ends, dst[r][:, :], apart[:, :], (S["dst_in"][r], 16 * (k + 1)))
                                act.sem_inc(S["picked"], 1)
                        slots(act, SILU, body)

                    @block.vector
                    def _(dve):
                        scattered, before = scatter.counters(dve), [counter(dve, f"{tag}_before", 0)]
                        dve.sem_inc(picks.used, 2)
                        number_nodes(None, dve, node_row, S["nodes"])
                        for g in range(2):
                            dve.memset(vals[g][:, :, :], 0.0)
                        dve.memset(hot[0][:, :, :], 0.0)
                        dve.memset(acc[:, :, :], 0.0).then_inc(S["sums_free"], 1)
                        dve.wait_ge(S["sums_free"], 1)
                        dve.memset(vals[1][:, :, D:D + 1], 1.0)
                        dve.memset(vals[0][:, :, D:D + 1], 1.0).then_inc(S["ones"], 1)
                        dve.wait_ge(S["affine_in"], 32)
                        dve.tensor_scalar(gamma[:, :], gamma[:, :], ROOT_K, None, ALU.mult).then_inc(S["affine_in"], 1)
                        dve.wait_ge(S["affine_in"], 33)
                        done = chain(dve, S["beta_step"], 0)
                        done(dve.memset(ones_b[:, :], 1.0))
                        split_parts(dve, done, beta[:, :], [beta_parts[:, p, :] for p in range(3)])
                        done(dve.tensor_scalar(beta_rows[:, :], beta_parts[:, 0, :], ident[:, 0:1], None, ALU.mult))
                        for p in (1, 2):
                            done(dve.scalar_tensor_tensor(beta_rows[:, :], beta_parts[:, p, :], ident[:, p:p + 1], beta_rows[:, :], ALU.mult, ALU.add))

                        def body(stage):
                            if stage(VARIANCE):
                                s, r, k = stage(VARIANCE)
                                dve.wait_ge(S["sq"], s + 1)
                                dve.tensor_reduce(var[:, r % 2, :], sq[r % 2][:, :].rearrange("p (a c) -> p a c", c=GC), AX.X, ALU.add).then_inc(S["ssq"], 1)
                            steps = []
                            if stage(VARIANCE) and stage(VARIANCE)[1] % 2:
                                s, r, k = stage(VARIANCE)
                                dve.wait_ge(S["ssq"], s + 1)
                                steps = list(root_steps(dve, *(x[:, :, :].rearrange("p g c -> p (g c)") for x in (var, rstd[r // 2], root_t, root_p))))
                                base = ROOT_STEPS * (DEPTH // 2 * k + r // 2)

                            def root_step():
                                if steps:
                                    n = ROOT_STEPS - len(steps)
                                    if n:
                                        dve.wait_ge(S["root"], base + n)
                                    steps.pop(0)().then_inc(S["root"], 1)

                            root_step()
                            if stage(SCALE):
                                s, r, k = stage(SCALE)
                                wait(dve, S["root"], ROOT_STEPS * (DEPTH // 2 * k + r // 2 + 1))
                                wait(dve, S["y"], s - 1)
                                dve.tensor_tensor(y[r % 2][:, :, :].rearrange("p j (a c) -> p (j a) c", c=GC),
                                                  bank(MSG[r]).rearrange("p (a c) -> p a c", c=GC),
                                                  rstd[r // 2][:, r % 2, :].unsqueeze(2).to_broadcast([P] + grouped), ALU.mult).then_inc(S["scaled"], 1)
                            root_step()
                            ends = stage(SCATTER) and span("dve", stage(SCATTER)[0])[0]
                            if stage(SCALE):
                                dve.wait_ge(S["scaled"], s + 1)
                                dve.tensor_tensor(y[r % 2][:, :, :], y[r % 2][:, :, :], gamma[:, :].unsqueeze(1).to_broadcast([P, TILES, D]),
                                                  ALU.mult).then_inc(S["gained"], 1)
                            root_step()
                            root_step()
                            if stage(SCATTER):
                                s, r, k = stage(SCATTER)
                                scatter.names(dve, scattered, before, ends, s, r, node_row)
                            while steps:
                                root_step()
                        slots(dve, SCATTER, body)
                        q = value(dve, scattered[0], 1)
                        dve.wait_ge(S["sums"], q)
                        scatter.add(dve, q, before)

        def time_vector(tvec):
            with ExitStack() as st:
                def b(name, shape, dt=F32):
                    return st.enter_context(nc.sbuf_tensor(f"tv_{name}", shape, dt))

                n = TD // P
                emb, gate, spread = b("emb", [P, n]), b("gate", [P, n]), b("spread", [P, n, P])
                w, bias = b("w", [P, n, D]), b("bias", [P, D])
                loaded, gated, spread_done, product, vec_done = (
                    sem(f"tv_{x}") for x in ("loaded", "gated", "spread", "product", "vec"))
                with nc.Block() as block:
                    @block.sync
                    def _(sp):
                        sp.dma_start(emb[:, :], io["L0_gnn_t_emb"].rearrange("(p a) -> p a", a=n)).then_inc(loaded, 16)
                        sp.dma_start(w[:, :, :], io["L0_gnn_tm_w"].rearrange("(p a) c -> p a c", a=n)).then_inc(loaded, 16)
                        sp.dma_start(bias[:, :], row_vector("L0_gnn_tm_b")).then_inc(loaded, 16)

                    @block.scalar
                    def _(act):
                        act.wait_ge(loaded, 48)
                        act.activation(gate[:, :], emb[:, :], ACT.Silu).then_inc(gated, 1)

                    @block.vector
                    def _(dve):
                        dve.wait_ge(gated, 1)
                        dve.tensor_copy(spread[:, :, :], gate[:, :].unsqueeze(2).to_broadcast([P, n, P])).then_inc(spread_done, 1)
                        dve.wait_ge(product, 1)
                        dve.tensor_tensor(tvec[:, :], bank(0)[:, 0:D], bias[:, :], ALU.add).then_inc(vec_done, 1)

                    @block.tensor
                    def _(pe):
                        pe.wait_ge(spread_done, 1)
                        for a in range(n):
                            last = pe.matmul(bank(0)[:, 0:D], spread[:, a, :], w[:, a, :], start=(a == 0), stop=(a == n - 1))
                        last.then_inc(product, 1)

        def node_update(tag, weight, bias, gain, shift, then):
            attention = then == "out"
            LEAD = 3 if attention else 4
            STEPS = LEAD + 1 + 1 + ROOT_STEPS + 3 + (2 if attention else 1)
            with ExitStack() as st:
                def b(name, shape, dt=F32):
                    return st.enter_context(nc.sbuf_tensor(f"{tag}_{name}", shape, dt))

                w, bias_row, gain_row, shift_row = b("w", [P, D]), b("bias", [P, D]), b("gain", [P, D]), b("shift", [P, D])
                w_mean = b("w_mean", [P, 2, GROUPS])
                stage, hT, y, z, sq = (b(x, [P, CHUNK, D]) for x in ("stage", "hT", "y", "z", "sq"))
                extra = None if then == "time" else b("extra", [P, CHUNK, D])
                share, held = b("share", [P, CHUNK, HEADS]), b("held", [P, CHUNK, 1])
                var, rstd, root_t, root_p = (b(x, [P, CHUNK * GROUPS]) for x in ("var", "rstd", "root_t", "root_p"))
                biased = None if attention else b("biased", [P, CHUNK, D])
                loaded, ready, step, staged, centred, normed, finished, flipped, hT_done, product, squared, gated, x_in, stored, held_done, bias_done, paced = (
                    sem(f"{tag}_{x}") for x in ("loaded", "ready", "step", "staged", "centred", "normed", "finished", "flipped", "hT",
                                                "product", "squared", "gated", "x_in", "stored", "held", "biased", "paced"))
                trans, prod = banks(0, CC), banks(2, CC).rearrange("p (k c) -> p k c", c=D)
                flat = lambda t: t[:, :, :].rearrange("p k c -> p (k c)")
                grouped = lambda t: t.rearrange("p k (g c) -> p (k g) c", c=GC)
                with nc.Block() as block:
                    @block.sync
                    def _(sp):
                        sp.dma_start(w[:, :], io[weight]).then_inc(loaded, 16)
                        for row, name in ((bias_row, bias), (gain_row, gain), (shift_row, shift)):
                            sp.dma_start(row[:, :], row_vector(name)).then_inc(loaded, 16)
                        if then == "residual":
                            with sp.Fori(0, CHUNKS) as i:
                                hold(sp, finished, i + 1, paced)
                                sp.dma_start(extra[:, :, :], by_block(resid, i)).then_inc(x_in, 16)
                        if attention:
                            sp.sem_inc(stored, 16)

                            def x_chunk(i):
                                hold(sp, finished, i + 1, paced)
                                sp.dma_start(extra[:, :, :], by_block(io["x_rows"], i)).then_inc(x_in, 16)
                                hold(sp, finished, i + 2, paced)

                            full = N_NODES // P
                            by_node = out[0:full * P, :].rearrange("(b p) c -> p b c", p=P)
                            with sp.Fori(0, CHUNKS - 1) as i:
                                x_chunk(i)
                                sp.dma_start(by_node[:, bass.ds(CHUNK * i, CHUNK), :], y[:, :, :]).then_inc(stored, 16)
                            x_chunk(CHUNKS - 1)
                            sp.dma_start(by_node[:, full - CHUNK + 1:full, :], y[:, 0:CHUNK - 1, :]).then_inc(stored, 16)
                            sp.dma_start(out[full * P:N_NODES, :], y[0:N_NODES - full * P, CHUNK - 1, :]).then_inc(stored, 16)
                            sp.wait_ge(stored, 16 * (CHUNKS + 2))

                    @block.vector
                    def _(dve):
                        setup = chain(dve, ready, 0)
                        dve.wait_ge(loaded, 64)
                        for n, t in enumerate((w, bias_row)):
                            groups = t[:, :].rearrange("p (g c) -> p g c", c=GC)
                            setup(dve.tensor_reduce(w_mean[:, n, :], groups, AX.X, ALU.add))
                            setup(dve.tensor_scalar(w_mean[:, n, :], w_mean[:, n, :], -1.0 / GC, None, ALU.mult))
                            setup(dve.tensor_tensor(groups, groups, w_mean[:, n, :].unsqueeze(2).to_broadcast([P, GROUPS, GC]), ALU.add))
                        setup(dve.tensor_scalar(gain_row[:, :], gain_row[:, :], ROOT_K, None, ALU.mult))
                        dve.sem_inc(finished, 1)
                        dve.sem_inc(centred, 1)

                        def lead(i, done):
                            blocks = bass.ds(CHUNK * i, CHUNK)
                            if attention:
                                done(dve.tensor_scalar(share[:, :, :], acc[:, blocks, D:D + HEADS], 1e-6, None, ALU.max))
                                done(dve.reciprocal(share[:, :, :], share[:, :, :]))
                                done(dve.tensor_tensor(stage[:, :, :].rearrange("p k (a c) -> p k a c", c=HD),
                                                       acc[:, blocks, 0:D].rearrange("p k (a c) -> p k a c", c=HD),
                                                       share[:, :, :].unsqueeze(3).to_broadcast([P, CHUNK, HEADS, HD]), ALU.mult))
                            else:
                                count = acc[:, blocks, D:D + 1]
                                done(dve.tensor_scalar(held[:, :, :], count, 1.0, None, ALU.min))
                                dve.sem_inc(held_done, 1)
                                done(dve.tensor_scalar(share[:, :, 0:1], count, 1.0, None, ALU.max))
                                done(dve.reciprocal(share[:, :, 0:1], share[:, :, 0:1]))
                                done(dve.tensor_tensor(stage[:, :, :], acc[:, blocks, 0:D],
                                                       share[:, :, 0:1].to_broadcast([P, CHUNK, D]), ALU.mult))
                            dve.sem_inc(staged, 1)

                        def chunk(i, more):
                            done = chain(dve, step, LEAD + STEPS * i)
                            blocks = bass.ds(CHUNK * i, CHUNK)
                            if attention:
                                dve.wait_ge(stored, 16 * i + 16)
                            else:
                                dve.wait_ge(bias_done, i + 1)
                            dve.wait_ge(product, i + 1)
                            done(dve.tensor_tensor(y[:, :, :], prod, row_of(bias_row) if attention else biased[:, :, :], ALU.add))
                            dve.sem_inc(centred, 1)
                            if more:
                                lead(i + 1, done)
                            dve.wait_ge(squared, i + 1)
                            done(dve.tensor_reduce(var[:, :], grouped(sq[:, :, :]), AX.X, ALU.add))
                            for root_step in root_steps(dve, var[:, :], rstd[:, :], root_t[:, :], root_p[:, :]):
                                done(root_step())
                            done(dve.tensor_tensor(grouped(y[:, :, :]), grouped(y[:, :, :]),
                                                   rstd[:, :].unsqueeze(2).to_broadcast([P, CHUNK * GROUPS, GC]), ALU.mult))
                            done(dve.tensor_tensor(y[:, :, :], y[:, :, :], row_of(gain_row), ALU.mult))
                            done(dve.tensor_tensor(y[:, :, :], y[:, :, :], row_of(shift_row), ALU.add))
                            dve.sem_inc(normed, 1)
                            if attention:
                                done(dve.tensor_tensor(y[:, :, :], y[:, :, :], hidden[:, blocks, :], ALU.add))
                            else:
                                dve.wait_ge(gated, i + 1)
                            if then != "time":
                                dve.wait_ge(x_in, 16 * (i + 1))
                            if then == "time":
                                done(dve.tensor_tensor(hidden[:, blocks, :], z[:, :, :], row_of(tvec), ALU.add))
                            elif then == "residual":
                                done(dve.tensor_tensor(hidden[:, blocks, :], z[:, :, :], extra[:, :, :], ALU.add))
                            else:
                                done(dve.tensor_tensor(y[:, :, :], y[:, :, :], extra[:, :, :], ALU.add))
                            dve.sem_inc(finished, 1)

                        lead(0, chain(dve, step, 0))
                        with dve.Fori(0, CHUNKS - 1) as i:
                            chunk(i, True)
                        chunk(CHUNKS - 1, False)

                    @block.gpsimd
                    def _(pool):
                        if not attention:
                            pool.wait_ge(ready, 7)
                            with pool.Fori(0, CHUNKS) as i:
                                pool.wait_ge(held_done, i + 1)
                                pool.wait_ge(centred, i + 1)
                                pool.tensor_tensor(biased[:, :, :], row_of(bias_row), held[:, :, :].to_broadcast([P, CHUNK, D]), ALU.mult).then_inc(bias_done, 1)

                    @block.tensor
                    def _(pe):
                        pe.wait_ge(ready, 7)
                        with pe.Fori(0, CHUNKS) as i:
                            pe.wait_ge(staged, i + 1)
                            for k in range(CHUNK):
                                last = pe.transpose(trans[:, k * D:(k + 1) * D], stage[:, k, :], ident[:, :])
                            last.then_inc(flipped, 1)
                            pe.wait_ge(hT_done, i + 1)
                            for k in range(CHUNK):
                                last = pe.matmul(prod[:, k, :], hT[:, k, :], w[:, :], start=True, stop=True)
                            last.then_inc(product, 1)

                    @block.scalar
                    def _(act):
                        with act.Fori(0, CHUNKS) as i:
                            act.wait_ge(flipped, i + 1)
                            act.activation(flat(hT), trans, ACT.Copy).then_inc(hT_done, 1)
                            act.wait_ge(centred, i + 2)
                            act.activation(sq[:, :, :], y[:, :, :], ACT.Square, scale=GC ** -0.5).then_inc(squared, 1)
                            if not attention:
                                act.wait_ge(normed, i + 1)
                                act.activation(z[:, :, :], y[:, :, :], ACT.Silu).then_inc(gated, 1)

        def logits_pass():
            with ExitStack() as st:
                def b(name, shape, dt=F32):
                    return st.enter_context(nc.sbuf_tensor(f"lg_{name}", shape, dt))

                def b2(name, shape, dt=F32):
                    return [b(f"{name}{g}", shape, dt) for g in range(2)]

                def deep(name, shape, dt=F32):
                    return [b(f"{name}{r}", shape, dt) for r in range(DEPTH)]

                idx, ea, digits = deep("idx", [P, TILES], I32), deep("ea", [ED + 1, SUPER]), deep("digits", [2, SUPER], BF16)
                rows = deep("rows", [P, TILES, 2 * D])
                zeros = b("zeros", [2, SUPER], BF16)
                picks = Picks("lg", b("pick", [P, 2, SUPER], BF16))
                prod, dots = b("prod", [P, TILES, D]), b("dots", [P, TILES * HEADS])
                lg, lg_wide = b2("lg", [P, TILES * HEADS]), b2("lg_wide", [P, TILES, P])
                top, w_ea = b("top", [P, 2]), b("w_ea", [ED + 1, HEADS])
                spare = [acc[:, :, :].rearrange("p b c -> p (b c)")[:, n * SUPER:(n + 1) * SUPER] for n in range(DEPTH + 5)]
                dst, masked, far, apart = spare[:DEPTH], spare[DEPTH:DEPTH + 2], spare[DEPTH + 2:DEPTH + 4], spare[DEPTH + 4]
                S = edge_sems("lg", ("set", "weights", "sp_paced", "pool_paced", "act_paced",
                                     "dve_paced", "dst_again", "query", "prod", "dots", "logits", "wide", "kept", "spread",
                                     "far", "top", "top_kept", "windows", "topped"),
                              ("idx_in", "dst_in", "digits_in", "ea_in", "rows_in", "v_out"))
                QUERY, EDGE, AGAIN, WIDE = (0, 1), (2, 3), (4, 5), (6, 7)
                PROJECT, LOGIT, WIDEN, SPREAD, TOP = 1, 2, 3, 4, 5
                with nc.Block() as block:
                    @block.sync
                    def _(sp):
                        sp.dma_start(w_ea[0:ED, :], io["L0_gnn_ew"]).then_inc(S["weights"], 16)
                        sp.dma_start(w_ea[ED:ED + 1, :], io["L0_gnn_eb"].rearrange("(a n) -> a n", a=1)).then_inc(S["weights"], 16)
                        sp.wait_ge(S["set"], 1)

                        def body(stage):
                            if stage(0):
                                s, r, k = stage(0)
                                hold(sp, S["rows_in"][r], 16 * TILES * k, S["sp_paced"])
                                sp.dma_start(idx[r][:, :], io["src_idx"][bass.ds(s, 1), :, :].rearrange("a p j -> (a p) j")).then_inc(S["idx_in"][r], 16)
                                hold(sp, S["query"], s - (DEPTH - 1), S["sp_paced"])
                                sp.dma_start(dst[r], dst_rows[bass.ds(s, 1), :].to_broadcast([P, SUPER])).then_inc(S["dst_in"][r], 16)
                                sp.dma_start(ea[r][0:ED, :], io["ea_rows"][:, bass.ds(s * SUPER, SUPER)]).then_inc(S["ea_in"][r], 16)
                            if stage(2):
                                s, r, k = stage(2)
                                hold(sp, S["dst_again"], s - (DEPTH - 1), S["sp_paced"])
                                sp.dma_start(digits[r][:, :], dst_digits[:, bass.ds(s * SUPER, SUPER)]).then_inc(S["digits_in"][r], 16)
                                hold(sp, S["rows_in"][r], 16 * TILES * (k + 1), S["sp_paced"])
                                sp.dma_start(v_edges[bass.ds(s, 1), :, :].rearrange("a p (j c) -> (a p) j c", c=D),
                                             rows[r][:, :, D:2 * D]).then_inc(S["v_out"][r], 16)
                        slots(sp, 2, body)
                        for r in range(DEPTH):
                            sp.wait_ge(S["v_out"][r], 16 * ITERS)

                    @block.gpsimd
                    def _(pool):
                        def body(stage):
                            s, r, k = stage(0)
                            hold(pool, S["idx_in"][r], 16 * (k + 1), S["pool_paced"])
                            hold(pool, S["prod"], s - (DEPTH - 1), S["pool_paced"])
                            hold(pool, S["v_out"][r], 16 * k, S["pool_paced"])
                            for j in range(TILES):
                                pool.indirect_dma_start(
                                    rows[r][:, j, :], None, kv_table,
                                    bass.IndirectOffsetOnAxis(idx[r][:, j:j + 1], 0)).then_inc(S["rows_in"][r], 16)
                        slots(pool, 0, body)

                    @block.tensor
                    def _(pe):
                        picked = picks.counters(pe)
                        pe.wait_ge(S["weights"], 32)
                        pe.wait_ge(S["set"], 1)

                        def body(stage):
                            near = stage(PROJECT) and span("pe", stage(PROJECT)[0])[0]
                            if stage(PROJECT):
                                s, r, k = stage(PROJECT)
                                wait(pe, S["logits"], s - 1)
                                pe.matmul(bank(QUERY[r % 2]), digit_w[:, :], zeros[:, :], start=True, stop=False, skip_group_check=True)
                                pick_pe(pe, picks, picked, near, bank(QUERY[r % 2]).rearrange("p (j c) -> p j c", c=D), parts_of_dst)
                                pe.wait_ge(S["ea_in"][r], 16 * (k + 1))
                                for j in range(TILES):
                                    last = pe.matmul(bank(EDGE[r % 2])[:, j * HEADS:(j + 1) * HEADS], ea[r][:, j * P:(j + 1) * P], w_ea[:, :],
                                                     start=(j == 0), stop=(j == TILES - 1), skip_group_check=True)
                                last.then_inc(S["query"], 1)
                            if stage(SPREAD):
                                s, r, k = stage(SPREAD)
                                wait(pe, S["windows"], s - 1)
                                pe.wait_ge(S["digits_in"][r], 16 * (k + 1))
                                pe.matmul(bank(AGAIN[r % 2]), digit_w[:, :], digits[r][:, :], start=True, stop=True).then_inc(S["dst_again"], 1)
                                pe.wait_ge(S["wide"], s + 1)
                                wait(pe, S["topped"], s - 1)
                                for j in range(TILES):
                                    last = pe.matmul(bank(WIDE[r % 2])[:, j * P:(j + 1) * P], lg_wide[r % 2][:, j, :], ident[:, :],
                                                     start=(j == 0), stop=(j == TILES - 1), skip_group_check=True)
                                last.then_inc(S["spread"], 1)
                        slots(pe, SPREAD, body)

                    @block.scalar
                    def _(act):
                        seen, picked = counter(act, "lg_seen", 1), picks.counters(act)
                        act.sem_inc(picks.made, 1)

                        def body(stage):
                            win_ends = stage(TOP) and span("act", stage(TOP)[0])[1]
                            if stage(TOP):
                                s, r, k = stage(TOP)

                                def couple(w):
                                    q = value(act, seen, 1, WINDOWS * SUPERS)
                                    act.wait_ge(S["dst_again"], s + 1)
                                    for h in range(2):
                                        hold(act, S["top"], 2 * q - 1 + h, S["act_paced"])
                                        act.activation(far[h], bank(AGAIN[r % 2]), ACT.Square, bias=neg_win[:, bass.ds(w + h, 1)], scale=PEN).then_inc(S["far"], 1)
                                    act.reg_add(seen, seen, 1)
                                pairs(act, win_ends, couple, 2)
                            if stage(WIDEN):
                                s, r, k = stage(WIDEN)
                                act.wait_ge(S["logits"], s + 1)
                                wait(act, S["spread"], s - 1)
                                act.activation(lg_wide[r % 2][:, :, :].rearrange("p j (h n) -> p (j h) n", n=WIN),
                                               lg[r % 2][:, :].unsqueeze(2).to_broadcast([P, TILES * HEADS, WIN]), ACT.Copy).then_inc(S["wide"], 1)
                            if stage(0):
                                s, r, k = stage(0)
                                pick_act(act, S, picks, picked, span("act", s)[0], dst[r], apart, (S["dst_in"][r], 16 * (k + 1)))
                            if stage(TOP):
                                act.wait_ge(S["far"], 2 * value(act, seen, 1, WINDOWS * SUPERS) - 2)
                                act.sem_inc(S["windows"], 1)
                        slots(act, TOP, body)

                    @block.vector
                    def _(dve):
                        seen, before = counter(dve, "lg_seen", 1), counter(dve, "lg_before", 0)
                        dve.sem_inc(picks.used, 2)
                        dve.sem_inc(S["top"], 2)
                        dve.sem_inc(S["top_kept"], 1)
                        dve.memset(top[:, :], NEG)
                        for r in range(DEPTH):
                            dve.memset(ea[r][:, :], 1.0)
                        dve.memset(zeros[:, :], 0.0)
                        dve.memset(tops[:, :], NEG).then_inc(S["set"], 1)
                        dve.wait_ge(S["set"], 1)

                        def keep_top(q):
                            dve.wait_ge(S["top"], 2 * q)
                            to = tops[:, bass.ds(value(dve, before, 0, WINDOWS - 1), 2)]
                            dve.tensor_tensor(to, to, top[:, :], ALU.max).then_inc(S["top_kept"], 1)

                        def body(stage):
                            if stage(LOGIT):
                                s, r, k = stage(LOGIT)
                                dve.wait_ge(S["query"], s + 1)
                                dve.wait_ge(S["rows_in"][r], 16 * TILES * (k + 1))
                                dve.tensor_tensor(prod[:, :, :], bank(QUERY[r % 2]).rearrange("p (j c) -> p j c", c=D),
                                                  rows[r][:, :, 0:D], ALU.mult).then_inc(S["prod"], 1)
                            if stage(TOP + 1):
                                dve.wait_ge(S["top"], 2 * value(dve, seen, 1, WINDOWS * SUPERS))
                                dve.sem_inc(S["topped"], 1)
                            win_ends = stage(TOP) and span("dve", stage(TOP)[0])[1]
                            if stage(LOGIT):
                                s, r, k = stage(LOGIT)
                                dve.wait_ge(S["prod"], s + 1)
                                dve.tensor_reduce(dots[:, :], prod[:, :, :].rearrange("p j (h c) -> p (j h) c", c=HD), AX.X, ALU.add).then_inc(S["dots"], 1)
                                dve.wait_ge(S["dots"], s + 1)
                                wait(dve, S["kept"], s - 1)
                                wait(dve, S["wide"], s - 1)
                                dve.scalar_tensor_tensor(lg[r % 2][:, :], dots[:, :], HD ** -0.5, bank(EDGE[r % 2])[:, 0:TILES * HEADS],
                                                         ALU.mult, ALU.add).then_inc(S["logits"], 1)
                            if stage(TOP):
                                s, r, k = stage(TOP)

                                def couple(w):
                                    q = value(dve, seen, 1, WINDOWS * SUPERS)
                                    keep_top(q)
                                    dve.wait_ge(S["spread"], s + 1)
                                    dve.wait_ge(S["top_kept"], q + 1)
                                    for h in range(2):
                                        hold(dve, S["far"], 2 * q - 1 + h, S["dve_paced"])
                                        dve.tensor_tensor_reduce(masked[h], bank(WIDE[r % 2]), far[h], 1.0, NEG,
                                                                 ALU.subtract, ALU.max, top[:, h:h + 1]).then_inc(S["top"], 1)
                                    dve.reg_mov(before, w)
                                    dve.reg_add(seen, seen, 1)
                                pairs(dve, win_ends, couple, 2)
                            if stage(LOGIT):
                                s, r, k = stage(LOGIT)
                                dve.wait_ge(S["logits"], s + 1)
                                dve.tensor_copy(logits[:, bass.ds(s, 1), :].rearrange("p a c -> p (a c)"), lg[r % 2][:, :]).then_inc(S["kept"], 1)
                        slots(dve, TOP + 1, body)
                        keep_top(value(dve, seen, 1, WINDOWS * SUPERS))

        def node_maxima():
            with ExitStack() as st:
                quarter = WINDOWS // 4
                by_window = st.enter_context(nc.sbuf_tensor("by_window", [quarter, 4, WIN, HEADS], F32))
                by_block_max = st.enter_context(nc.sbuf_tensor("max_by_block", [P, BLOCKS, HEADS], F32))
                flipped, moved, written, loaded, step = (sem(f"max_{x}") for x in ("flipped", "moved", "written", "loaded", "step"))
                with nc.Block() as block:
                    @block.tensor
                    def _(pe):
                        for a in range(4):
                            last = pe.transpose(bank(0)[0:quarter, a * P:(a + 1) * P], tops[:, a * quarter:(a + 1) * quarter], ident[:, :])
                        last.then_inc(flipped, 1)

                    @block.sync
                    def _(sp):
                        sp.wait_ge(moved, 1)
                        sp.dma_start(max_nodes.rearrange("(a w n) h -> w a (n h)", a=4, n=WIN),
                                     by_window[:, :, :, :].rearrange("w a n h -> w a (n h)")).then_inc(written, 16)
                        sp.wait_ge(written, 16)
                        sp.dma_start(by_block_max[:, :, :], max_nodes.rearrange("(b p) h -> p b h", p=P)).then_inc(loaded, 16)

                    @block.vector
                    def _(dve):
                        dve.wait_ge(flipped, 1)
                        for a in range(4):
                            last = dve.tensor_copy(by_window[:, a, :, :], bank(0)[0:quarter, a * P:(a + 1) * P].rearrange("w (h n) -> w n h", n=WIN))
                        last.then_inc(moved, 1)
                        dve.wait_ge(loaded, 16)
                        done = chain(dve, step, 0)
                        for p in range(3):
                            done(dve.tensor_copy(max_parts[:, :, p, :], by_block_max[:, :, :]))
                            if p < 2:
                                done(dve.tensor_tensor(by_block_max[:, :, :], by_block_max[:, :, :], max_parts[:, :, p, :], ALU.subtract))

        def softmax_pass():
            with ExitStack() as st:
                def b(name, shape, dt=F32):
                    return st.enter_context(nc.sbuf_tensor(f"sm_{name}", shape, dt))

                def b2(name, shape, dt=F32):
                    return [b(f"{name}{g}", shape, dt) for g in range(2)]

                def deep(name, shape, dt=F32):
                    return [b(f"{name}{r}", shape, dt) for r in range(DEPTH)]

                dst, v = deep("dst", [P, SUPER]), deep("v", [P, TILES, D])
                apart, picks = b("apart", [P, SUPER]), Picks("sm", b("pick", [P, 2, SUPER], BF16))
                zeros = b("zeros", [2, TILES * 3 * HEADS], BF16)
                below, highest, vals = b2("below", [P, TILES * HEADS]), b2("highest", [P, TILES * HEADS]), deep("vals", [P, TILES, ACC_W])
                hot = b2("hot", [P, TILES, P])
                node_row = dst_parts[:, :, :, :].rearrange("p b k c -> p (b k c)")[:, 0:2 * NODES].bitcast(F32).rearrange("p (b n) -> p b n", n=P)
                S = edge_sems("sm", ("set", "nodes", "picked", "hot", "sums", "sums_free", "sp_paced",
                                     "act_paced", "maxima", "maxima_used", "below", "weight", "vals", "vals_free"), ("dst_in", "v_in"))
                scatter = Scatter("sm", S, hot, ACC_W, 5)
                MAX = (0, 1)
                MAXIMUM, BELOW, LOAD_V, EXPONENT, WEIGHT, SCATTER = 1, 2, 2, 3, 4, 5
                with nc.Block() as block:
                    @block.sync
                    def _(sp):
                        def body(stage):
                            if stage(0):
                                s, r, k = stage(0)
                                hold(sp, S["picked"], s - (DEPTH - 1), S["sp_paced"])
                                sp.dma_start(dst[r][:, :], dst_rows[bass.ds(s, 1), :].to_broadcast([P, SUPER])).then_inc(S["dst_in"][r], 16)
                            if stage(LOAD_V):
                                s, r, k = stage(LOAD_V)
                                hold(sp, S["vals"], s - (DEPTH - 1), S["sp_paced"])
                                sp.dma_start(v[r][:, :, :], v_edges[bass.ds(s, 1), :, :].rearrange("a p (j c) -> (a p) j c", c=D)).then_inc(S["v_in"][r], 16)
                        slots(sp, LOAD_V, body)

                    @block.gpsimd
                    def _(pool):
                        number_nodes(pool, None, node_row, S["nodes"])

                    @block.tensor
                    def _(pe):
                        picked, scattered = picks.counters(pe), scatter.counters(pe)
                        kept = span_registers(pe, "sm")
                        pe.wait_ge(S["set"], 1)
                        pe.matmul(bank(SUMS[0])[:, 0:ACC_W], hot[0][:, 0, :], vals[0][:, 0, :], start=True, stop=True).then_inc(S["sums"], 1)

                        def body(stage):
                            far = stage(SCATTER) and kept_span(pe, kept[stage(SCATTER)[1]])
                            near = stage(MAXIMUM) and keep_span(pe, kept[stage(MAXIMUM)[1]], span("pe", stage(MAXIMUM)[0])[0])
                            if stage(SCATTER):
                                s, r, k = stage(SCATTER)
                                scatter.products(pe, scattered, far, r, vals[r], (S["vals"], s + 1))
                            if stage(MAXIMUM):
                                s, r, k = stage(MAXIMUM)
                                wait(pe, S["below"], s - 1)
                                maxima = bank(MAX[r % 2])[:, 0:TILES * 3 * HEADS]
                                pe.matmul(maxima, digit_w[:, :], zeros[:, :], start=True, stop=False, skip_group_check=True)
                                pick_pe(pe, picks, picked, near, maxima.rearrange("p (j c) -> p j c", c=3 * HEADS),
                                        lambda blk: [max_parts[:, bass.ds(blk, 1), :, :].rearrange("p a k c -> p (a k c)")])
                                pe.matmul(maxima, digit_w[:, :], zeros[:, :], start=False, stop=True,
                                          skip_group_check=True).then_inc(S["maxima"], 1)
                        slots(pe, SCATTER, body)

                    @block.scalar
                    def _(act):
                        picked = picks.counters(act)
                        act.sem_inc(picks.made, 1)

                        def body(stage):
                            ends = stage(0) and span("act", stage(0)[0])[0]
                            if stage(EXPONENT):
                                s, r, k = stage(EXPONENT)
                                act.wait_ge(S["below"], s + 1)
                                wait(act, S["vals_free"], s - (DEPTH - 1))
                                act.activation(vals[r][:, :, D:ACC_W], below[r % 2][:, :].rearrange("p (j h) -> p j h", h=HEADS),
                                               ACT.Exp).then_inc(S["weight"], 1)
                            if stage(0):
                                s, r, k = stage(0)
                                pick_act(act, S, picks, picked, ends, dst[r][:, :], apart[:, :], (S["dst_in"][r], 16 * (k + 1)))
                                act.sem_inc(S["picked"], 1)
                        slots(act, EXPONENT, body)

                    @block.vector
                    def _(dve):
                        scattered, before = scatter.counters(dve), [counter(dve, f"sm_before_{x}", 0) for x in ("block", "bank")]
                        dve.sem_inc(picks.used, 2)
                        number_nodes(None, dve, node_row, S["nodes"])
                        dve.memset(vals[0][:, :, :], 0.0)
                        dve.memset(hot[0][:, :, :], 0.0)
                        dve.memset(zeros[:, :], 0.0).then_inc(S["set"], 1)
                        dve.memset(acc[:, :, :], 0.0).then_inc(S["sums_free"], 1)
                        dve.wait_ge(S["sums_free"], 1)

                        def body(stage):
                            if stage(SCATTER):
                                s, r, k = stage(SCATTER)
                                scatter.names(dve, scattered, before, span("dve", s)[0], s, r, node_row)
                            if stage(BELOW):
                                s, r, k = stage(BELOW)
                                dve.wait_ge(S["maxima"], s + 1)
                                wait(dve, S["weight"], s - 1)
                                maxima = bank(MAX[r % 2])[:, 0:TILES * 3 * HEADS].rearrange("p (j k h) -> p j k h", k=3, h=HEADS)
                                under = below[r % 2][:, :].rearrange("p (j h) -> p j h", h=HEADS)
                                dve.tensor_reduce(highest[r % 2][:, :], maxima.rearrange("p j k h -> p j h k"), AX.X, ALU.add).then_inc(S["maxima_used"], 1)
                                dve.wait_ge(S["maxima_used"], s + 1)
                                dve.tensor_tensor(under, logits[:, bass.ds(s, 1), :].rearrange("p a (j h) -> p (a j) h", h=HEADS),
                                                  highest[r % 2][:, :].rearrange("p (j h) -> p j h", h=HEADS), ALU.subtract).then_inc(S["below"], 1)
                            if stage(WEIGHT):
                                s, r, k = stage(WEIGHT)
                                dve.wait_ge(S["weight"], s + 1)
                                dve.wait_ge(S["v_in"][r], 16 * (k + 1))
                                dve.tensor_tensor(vals[r][:, :, 0:D].rearrange("p j (h c) -> p j h c", c=HD),
                                                  v[r][:, :, :].rearrange("p j (h c) -> p j h c", c=HD),
                                                  vals[r][:, :, D:ACC_W].unsqueeze(3).to_broadcast([P, TILES, HEADS, HD]),
                                                  ALU.mult).then_inc(S["vals"], 1)
                        slots(dve, SCATTER, body)
                        q = value(dve, scattered[0], 1)
                        dve.wait_ge(S["sums"], q)
                        scatter.add(dve, q, before)

        project("tab1", [w_pair[0][:, 0, :], w_pair[0][:, 1, :]], [b1_row[0], None], src_table, stores=((kept, 16),))
        end_phase()
        conv("conv1", 0)
        end_phase()
        time_vector(tvec)
        end_phase()
        node_update("node1", "L0_gnn_c1_w2", "L0_gnn_c1_b2", "L0_gnn_n1_g", "L0_gnn_n1_b", "time")
        end_phase()
        project("tab2", [w_pair[1][:, 0, :], w_pair[1][:, 1, :]], [b1_row[1], None], src_table)
        end_phase()
        conv("conv2", 1)
        end_phase()
        node_update("node2", "L0_gnn_c2_w2", "L0_gnn_c2_b2", "L0_gnn_n2_g", "L0_gnn_n2_b", "residual")
        end_phase()
        project("tab3", [w_qkv[:, r, :] for r in range(3)], [b_qkv[r] for r in range(3)], kv_table)
        end_phase()
        with nc.sbuf_tensor("logits", [P, SUPERS, TILES * HEADS], F32) as logits, \
                nc.sbuf_tensor("max_parts", [P, BLOCKS, 3, HEADS], BF16) as max_parts:
            with nc.sbuf_tensor("tops", [P, WINDOWS + 1], F32) as tops:
                logits_pass()
                end_phase()
                node_maxima()
                end_phase()
            softmax_pass()
            end_phase()
        node_update("node3", "L0_gnn_ow", "L0_gnn_ob", "L0_gnn_an_g", "L0_gnn_an_b", "out")
        end_phase()


_OUT = ((N_NODES, D), "float32")


def kernel(**inputs):
    import concourse.bacc as bacc
    from concourse.bass_utils import run_bass_kernel_spmd

    a = {k: np.asarray(v) for k, v in inputs.items()}
    x = np.zeros((NODES, D), a["x"].dtype)
    x[:N_NODES] = a.pop("x")
    src = np.zeros(EDGES, np.int32)
    src[:N_EDGES] = a.pop("src")
    dst = np.full(EDGES, N_NODES, np.int32)
    dst[:N_EDGES] = a.pop("dst")
    ea = np.zeros((EDGES, ED), a["edge_attr_4"].dtype)
    ea[:N_EDGES] = a.pop("edge_attr_4")
    arrays = {"x_rows": x,
              "src_idx": src.reshape(SUPERS, TILES, P).transpose(0, 2, 1),
              "dst_rows": dst.reshape(SUPERS, SUPER),
              "dst_cols": dst.reshape(SUPERS * TILES, P).T,
              "ea_rows": ea.T, **a}
    arrays = {f"in_{k}": np.ascontiguousarray(v) for k, v in arrays.items()}
    nc = bacc.Bacc("TRN2", target_bir_lowering=False, num_devices=1)
    io = {k[3:]: nc.dram_tensor(k, v.shape, mybir.dt.from_np(v.dtype), kind="ExternalInput").ap() for k, v in arrays.items()}
    out = nc.dram_tensor("out", _OUT[0], F32, kind="ExternalOutput").ap()
    build(nc, io, out)
    result = run_bass_kernel_spmd(nc, [arrays], core_ids=[0])
    return np.asarray(result.results[0]["out"])
```
